# Optimizing a Trainium2 kernel written in Bass

```python
import numpy as np
import jax
import jax.numpy as jnp

def _softmax(x, axis=-1):
    return jax.nn.softmax(x, axis=axis)

def _gelu(x):
    return jax.nn.gelu(x, approximate=True)

def _silu(x):
    return jax.nn.silu(x)

def _sigmoid(x):
    return jax.nn.sigmoid(x)

def _layernorm(x, axis=-1, eps=1e-05):
    m = jnp.mean(x, axis=axis, keepdims=True)
    v = jnp.var(x, axis=axis, keepdims=True)
    return (x - m) / jnp.sqrt(v + eps)

def _scatter_add(tgt, idx, src, axis=0):
    return tgt.at[idx].add(src)

def _segment_sum(src, seg, n):
    return jax.ops.segment_sum(src, seg, n)
kernel_name = 'mk_decoder_postln_d1_seqx_r4_6a3bc6'

def setup_inputs(seed: int=0):
    np.random.seed(seed)
    _w = jnp.asarray

    def _rec_inputs():
        import jax
        import jax.numpy as jnp
        _rk = jax.random.key(seed)
        x = -0.0002928 + 1 * jax.random.normal(jax.random.fold_in(_rk, 1), (64, 128, 256), jnp.float32)
        _lenS = 128 - jax.random.randint(jax.random.fold_in(_rk, 7), (64,), 0, max(1, 128 // 4) + 1, jnp.int32)
        _lenS2 = 128 - jax.random.randint(jax.random.fold_in(_rk, 8), (64,), 0, max(1, 128 // 4) + 1, jnp.int32)
        _ctx_1024P = jax.random.normal(jax.random.fold_in(_rk, 11), (64, 16, 256), jnp.float32)
        _ctx_1024c = jax.random.dirichlet(jax.random.fold_in(_rk, 511), 0.3 * jnp.ones((16,), jnp.float32), (64, 128))
        _ctx_1024t = jnp.einsum('bsk,bkd->bsd', _ctx_1024c, _ctx_1024P)
        _ctx_1024t = _ctx_1024t * jax.lax.rsqrt(jnp.mean(jnp.square(_ctx_1024t)) + 1e-12) * 0.953939
        ctx_1024 = -1.39393e-06 + 0.999914 * (_ctx_1024t + 0.3 * jax.random.normal(jax.random.fold_in(_rk, 611), (64, 128, 256), jnp.float32))
        return (x, ctx_1024)
    x, ctx_1024 = _rec_inputs()

    def _L0_attn_setup():
        import jax, jax.numpy as jnp
        import numpy as np
        B, S, D, H = (4, 512, 256, 16)
        HD = D // H
        LB = 0.0
        EPS = 1e-05
        key = jax.random.key(seed)
        ks = jax.random.split(key, 8)
        s = 1.0 / np.sqrt(D)
        W = lambda k: jax.random.normal(k, (D, D), jnp.float32) * s
        return {'x': jax.random.normal(ks[0], (B, S, D), jnp.float32), 'Wq': W(ks[1]), 'Wk': W(ks[2]), 'Wv': W(ks[3]), 'Wf': W(ks[4]), 'bf': jnp.zeros((D,), jnp.float32), 'Wg': W(ks[5]), 'Wout': W(ks[6]), 'gamma': jnp.ones((D,), jnp.float32), 'beta': jnp.zeros((D,), jnp.float32)}
    _L0_attn_all = _L0_attn_setup()
    _L0_attn_in = {k: v for k, v in _L0_attn_all.items() if k in ('Wq', 'Wk', 'Wv', 'Wf', 'bf', 'Wg', 'Wout', 'gamma', 'beta')}
    del _L0_attn_all

    def _L0_xattn_setup():
        import jax, jax.numpy as jnp
        import numpy as np
        import math
        EMBED_DIM = 256
        NUM_HEADS = 16
        HEAD_DIM = EMBED_DIM // NUM_HEADS
        SCALE = math.sqrt(HEAD_DIM)
        key = jax.random.key(seed)
        ks = jax.random.split(key, 12)
        B, S, D = (2, 512, EMBED_DIM)
        s = 1.0 / math.sqrt(D)
        return {'query': jax.random.normal(ks[0], (B, S, D), jnp.float32), 'key': jax.random.normal(ks[1], (B, S, D), jnp.float32), 'value': jax.random.normal(ks[2], (B, S, D), jnp.float32), 'Wq': jax.random.normal(ks[3], (D, D), jnp.float32) * s, 'bq': jax.random.normal(ks[4], (D,), jnp.float32) * 0.01, 'Wk': jax.random.normal(ks[5], (D, D), jnp.float32) * s, 'bk': jax.random.normal(ks[6], (D,), jnp.float32) * 0.01, 'Wv': jax.random.normal(ks[7], (D, D), jnp.float32) * s, 'bv': jax.random.normal(ks[8], (D,), jnp.float32) * 0.01, 'Wo': jax.random.normal(ks[9], (D, D), jnp.float32) * s, 'bo': jax.random.normal(ks[10], (D,), jnp.float32) * 0.01}
    _L0_xattn_all = _L0_xattn_setup()
    _L0_xattn_in = {k: v for k, v in _L0_xattn_all.items() if k in ('Wq', 'bq', 'Wk', 'bk', 'Wv', 'bv', 'Wo', 'bo')}
    del _L0_xattn_all

    def _L0_ffn_setup():
        import jax, jax.numpy as jnp
        import numpy as np
        BLOCK = 32
        W_BITS = 4
        ACT_BITS = 16

        def act_qdq(x):
            qmax = 2.0 ** (ACT_BITS - 1) - 1.0
            scale = jnp.maximum(jnp.max(jnp.abs(x)) / qmax, 1e-12)
            return jnp.clip(jnp.round(x / scale), -qmax - 1.0, qmax) * scale

        def fixed_qdq_u16(x):
            scale = 1.0 / 65536.0
            return jnp.clip(jnp.round(x / scale), 0.0, 65535.0) * scale

        def lpbq_dequant(w):
            O, I = w.shape
            qmax = 2.0 ** (W_BITS - 1) - 1.0
            wb = w.reshape(O, I // BLOCK, BLOCK)
            s = jnp.maximum(jnp.max(jnp.abs(wb), axis=-1, keepdims=True) / qmax, 1e-12)
            wq = jnp.clip(jnp.round(wb / s), -qmax - 1.0, qmax) * s
            return wq.reshape(O, I)
        key = jax.random.key(seed)
        k1, k2, k3, k4 = jax.random.split(key, 4)
        B, S, H, I = (2, 1024, 256, 768)
        x = jax.random.normal(k1, (B, S, H), jnp.float32)
        w_gate = jax.random.normal(k2, (I, H), jnp.float32) * 0.02
        w_up = jax.random.normal(k3, (I, H), jnp.float32) * 0.02
        w_down = jax.random.normal(k4, (H, I), jnp.float32) * 0.02
        return {'x': x, 'w_gate': w_gate, 'w_up': w_up, 'w_down': w_down}
    _L0_ffn_all = _L0_ffn_setup()
    _L0_ffn_in = {k: v for k, v in _L0_ffn_all.items() if k in ('w_gate', 'w_up', 'w_down')}
    del _L0_ffn_all
    return {'x': x, 'ctx_1024': ctx_1024, 'L0_attn_Wq': _L0_attn_in['Wq'], 'L0_attn_Wk': _L0_attn_in['Wk'], 'L0_attn_Wv': _L0_attn_in['Wv'], 'L0_attn_Wf': _L0_attn_in['Wf'], 'L0_attn_bf': _L0_attn_in['bf'], 'L0_attn_Wg': _L0_attn_in['Wg'], 'L0_attn_Wout': _L0_attn_in['Wout'], 'L0_attn_gamma': _L0_attn_in['gamma'], 'L0_attn_beta': _L0_attn_in['beta'], 'L0_xattn_Wq': _L0_xattn_in['Wq'], 'L0_xattn_bq': _L0_xattn_in['bq'], 'L0_xattn_Wk': _L0_xattn_in['Wk'], 'L0_xattn_bk': _L0_xattn_in['bk'], 'L0_xattn_Wv': _L0_xattn_in['Wv'], 'L0_xattn_bv': _L0_xattn_in['bv'], 'L0_xattn_Wo': _L0_xattn_in['Wo'], 'L0_xattn_bo': _L0_xattn_in['bo'], 'L0_ffn_w_gate': _L0_ffn_in['w_gate'], 'L0_ffn_w_up': _L0_ffn_in['w_up'], 'L0_ffn_w_down': _L0_ffn_in['w_down']}

def reference(x, ctx_1024, L0_attn_Wq, L0_attn_Wk, L0_attn_Wv, L0_attn_Wf, L0_attn_bf, L0_attn_Wg, L0_attn_Wout, L0_attn_gamma, L0_attn_beta, L0_xattn_Wq, L0_xattn_bq, L0_xattn_Wk, L0_xattn_bk, L0_xattn_Wv, L0_xattn_bv, L0_xattn_Wo, L0_xattn_bo, L0_ffn_w_gate, L0_ffn_w_up, L0_ffn_w_down):
    import jax
    import jax.numpy as jnp

    def _L0_attn_ref(x, Wq, Wk, Wv, Wf, bf, Wg, Wout, gamma, beta):
        import jax, jax.numpy as jnp
        import numpy as np
        B, S, D, H = (4, 512, 256, 16)
        HD = D // H
        LB = 0.0
        EPS = 1e-05
        b, s, d = x.shape
        q = (x @ Wq).reshape(b, s, H, HD)
        k = (x @ Wk).reshape(b, s, H, HD)
        v = (x @ Wv).reshape(b, s, H, HD)
        fg = jax.nn.sigmoid(x @ Wf + bf).reshape(b, s, H, HD)
        fg = LB + (1.0 - LB) * fg
        qs, ks_, vs, gs = (jnp.moveaxis(t, 1, 0) for t in (q, k, v, fg))

        def step(state, inp):
            qt, kt, vt, gt = inp
            state = state * gt[..., None] + vt[..., None] * kt[..., None, :]
            out_t = jnp.einsum('bhij,bhj->bhi', state, qt)
            return (state, out_t)
        state0 = jnp.zeros((b, H, HD, HD), x.dtype)
        _, outs = jax.lax.scan(step, state0, (qs, ks_, vs, gs))
        out = jnp.moveaxis(outs, 0, 1).reshape(b, s, d)
        mu = out.mean(-1, keepdims=True)
        var = out.var(-1, keepdims=True)
        out = (out - mu) * jax.lax.rsqrt(var + EPS) * gamma + beta
        out = out * jax.nn.silu(x @ Wg)
        return out @ Wout

    def _L0_xattn_ref(query, key, value, Wq, bq, Wk, bk, Wv, bv, Wo, bo):
        import jax, jax.numpy as jnp
        import numpy as np
        import math
        EMBED_DIM = 256
        NUM_HEADS = 16
        HEAD_DIM = EMBED_DIM // NUM_HEADS
        SCALE = math.sqrt(HEAD_DIM)
        B, S, D = query.shape
        H, Hd = (NUM_HEADS, HEAD_DIM)

        def proj(x, W, b):
            return (x @ W.T + b).reshape(B, S, H, Hd).transpose(0, 2, 1, 3)
        Q = proj(query, Wq, bq)
        K = proj(key, Wk, bk)
        V = proj(value, Wv, bv)
        scores = jnp.einsum('bhqd,bhkd->bhqk', Q, K) / SCALE
        attn = jax.nn.softmax(scores, axis=-1)
        out = jnp.einsum('bhqk,bhkd->bhqd', attn, V)
        out = out.transpose(0, 2, 1, 3).reshape(B, S, D)
        return out @ Wo.T + bo

    def _L0_ffn_ref(x, w_gate, w_up, w_down):
        import jax, jax.numpy as jnp
        import numpy as np
        BLOCK = 32
        W_BITS = 4
        ACT_BITS = 16

        def act_qdq(x):
            qmax = 2.0 ** (ACT_BITS - 1) - 1.0
            scale = jnp.maximum(jnp.max(jnp.abs(x)) / qmax, 1e-12)
            return jnp.clip(jnp.round(x / scale), -qmax - 1.0, qmax) * scale

        def fixed_qdq_u16(x):
            scale = 1.0 / 65536.0
            return jnp.clip(jnp.round(x / scale), 0.0, 65535.0) * scale

        def lpbq_dequant(w):
            O, I = w.shape
            qmax = 2.0 ** (W_BITS - 1) - 1.0
            wb = w.reshape(O, I // BLOCK, BLOCK)
            s = jnp.maximum(jnp.max(jnp.abs(wb), axis=-1, keepdims=True) / qmax, 1e-12)
            wq = jnp.clip(jnp.round(wb / s), -qmax - 1.0, qmax) * s
            return wq.reshape(O, I)
        x = act_qdq(x)
        up = act_qdq(x @ lpbq_dequant(w_up).T)
        gate = act_qdq(x @ lpbq_dequant(w_gate).T)
        sig = fixed_qdq_u16(jax.nn.sigmoid(gate))
        gate = act_qdq(gate * sig)
        o = act_qdq(gate * up)
        return o @ lpbq_dequant(w_down).T
    x = _layernorm(x + _L0_attn_ref(x, L0_attn_Wq, L0_attn_Wk, L0_attn_Wv, L0_attn_Wf, L0_attn_bf, L0_attn_Wg, L0_attn_Wout, L0_attn_gamma, L0_attn_beta), axis=-1)
    x = _layernorm(x + _L0_xattn_ref(x, ctx_1024, ctx_1024, L0_xattn_Wq, L0_xattn_bq, L0_xattn_Wk, L0_xattn_bk, L0_xattn_Wv, L0_xattn_bv, L0_xattn_Wo, L0_xattn_bo), axis=-1)
    x = _layernorm(x + _L0_ffn_ref(x, L0_ffn_w_gate, L0_ffn_w_up, L0_ffn_w_down), axis=-1)
    return x

_drawn_inputs = setup_inputs


def setup_inputs(seed=0):
    import zlib

    import numpy as np

    out = dict(_drawn_inputs(seed))
    spreads = {'L0_attn_bf': (0.0, 0.497), 'L0_attn_gamma': (1.0, 0.2), 'L0_attn_beta': (0.0, 0.1)}
    factors = {'L0_xattn_bq': 27.777, 'L0_xattn_bk': 64.0, 'L0_xattn_bv': 6.8, 'L0_xattn_bo': 6.248}
    for name, (base, spread) in spreads.items():
        noise = np.random.default_rng([zlib.crc32(name.encode()), seed]).standard_normal(out[name].shape)
        drawn = base * np.exp(spread * noise) if base else spread * noise
        out[name] = jnp.asarray(drawn.astype(out[name].dtype))
    for name, factor in factors.items():
        out[name] = (out[name] * factor).astype(out[name].dtype)
    return out
```

```python
from contextlib import ExitStack

import concourse.bass as bass
from concourse import mybir

ALU = mybir.AluOpType
ACT = mybir.ActivationFunctionType
AX = mybir.AxisListType
F32 = mybir.dt.float32
F16 = mybir.dt.float16
BF16 = mybir.dt.bfloat16
I16 = mybir.dt.int16
RMAX = bass.bass_isa.ReduceOp.max

P = 128
B, S, D = 64, 128, 256
H, HD = 16, 16
KC = D // P
HALF = 2
HH = H // HALF
FF = 768
FC = FF // P
QBLOCK = 32
EPS = 1e-5
MAGIC = 12582912.0
MAGIC16 = 192.0
QMAX = 32767.0
TINY = 1e-12
SIG_TOP = 65535.0 / 65536.0


class Chain:

    def __init__(self, eng, sem, start=0):
        self.eng, self.sem, self.start, self.n = eng, sem, start, 0

    def did(self, ins):
        ins.then_inc(self.sem, 1)
        self.n += 1

    def wait(self):
        self.eng.wait_ge(self.sem, self.start + self.n)

    def wait_apart(self, seen):
        self.wait()
        self.eng.sem_inc(seen, 1)


def wait_if(eng, sem, value):
    if not (isinstance(value, int) and value <= 0):
        eng.wait_ge(sem, value)


def setup_block(nc, t, w):
    with ExitStack() as ctx:
        def sb(name, shape, dt=F32):
            return ctx.enter_context(nc.sbuf_tensor(name, shape, dt))

        def sem(name):
            return ctx.enter_context(nc.semaphore(name))

        XW = ["xq", "xk", "xv", "xo"]
        raw = sb("raw_xattn", [P, 4, KC, D])
        rawf = sb("raw_ff", [P, 2, FC, D])
        rawd = sb("raw_down", [P, KC, FF])
        NB_U, NB_D = D // QBLOCK, FF // QBLOCK
        su = sb("scale_u", [P, 2 * FC * NB_U])
        ru = sb("rscale_u", [P, 2 * FC * NB_U])
        sd = sb("scale_d", [P, KC * NB_D])
        rd = sb("rscale_d", [P, KC * NB_D])
        cu = sb("rowmax_u_inv", [P, 2 * FC])
        cd = sb("rowmax_d_inv", [P, KC])
        cdm = sb("rowmax_d", [P, KC])
        cdt = sb("rowmax_d_row", [1, D])
        ones = sb("ones_row", [1, P])
        tps = [ctx.enter_context(nc.psum_tensor(f"setup_ps{i}", [P, 512], F32)) for i in range(2)]

        loaded = sem("setup_loaded")
        ident_set = sem("ident_set")
        vec = sem("setup_vec")
        quantised = sem("setup_quantised")
        turned = sem("setup_turned")
        taken = sem("setup_taken")
        row_made = sem("setup_row_made")

        NT = 16 // 4 + 2 * FC * KC // 4 + KC * FC // 4
        with nc.Block() as block:

            @block.sync
            def _(sp):
                for i, name in enumerate(XW):
                    sp.dma_start(raw[:, i], w[name].rearrange("(c p) d -> p c d", p=P)).then_inc(loaded, 16)
                sp.dma_start(rawf[:, 0], w["up"].rearrange("(c p) d -> p c d", p=P)).then_inc(loaded, 16)
                sp.dma_start(rawf[:, 1], w["gate"].rearrange("(c p) d -> p c d", p=P)).then_inc(loaded, 16)
                sp.dma_start(rawd[:], w["down"].rearrange("(c p) d -> p c d", p=P)).then_inc(loaded, 16)
                for kc in range(KC):
                    rows = slice(kc * P, (kc + 1) * P)
                    for i, name in enumerate(["q", "k", "v", "f"]):
                        sp.dma_start(t["w_rec"][:, kc, :, i, :],
                                     w[name][rows].rearrange("p (h c) -> p h c", h=HALF)).then_inc(loaded, 16)
                    sp.dma_start(t["w_g"][:, kc, :], w["g"][rows]).then_inc(loaded, 16)
                    sp.dma_start(t["w_out"][:, kc, :], w["out"][rows]).then_inc(loaded, 16)
                sp.dma_start(t["bf_row"][:], w["bf"].rearrange("(a d) -> a d", a=1)).then_inc(loaded, 16)
                for dst, src in (("gamma", "gamma"), ("beta", "beta"), ("bq", "bq"), ("bk", "bk")):
                    sp.dma_start(t[dst][:], w[src].rearrange("(c p) -> p c", p=P), allow_slow_non_contiguous=True).then_inc(loaded, 16)
                for dst in ("bv", "bo"):
                    sp.dma_start(t[dst][:], w[dst].partition_broadcast(P)).then_inc(loaded, 16)
                sp.wait_ge(loaded, 16 * 26)

            @block.gpsimd
            def _(pool):
                nc.gpsimd.memset(t["ident"][:], 0.0).then_inc(ident_set, 1)
                pool.wait_ge(ident_set, 1)
                nc.gpsimd.affine_select(out=t["ident"][:], in_=t["ident"][:], compare_op=ALU.not_equal, fill=1.0,
                                        base=0, pattern=[[-1, P]], channel_multiplier=1).then_inc(ident_set, 1)

            @block.vector
            def _(dve):
                V = nc.vector
                c = Chain(dve, vec)
                dve.wait_ge(ident_set, 2)
                dve.wait_ge(loaded, 16 * 26)
                ident = t["ident"]
                c.did(V.tensor_copy(t["ident_b"][:], ident[:]))
                c.did(V.tensor_copy(t["ident_h"][:], ident[:]))
                c.did(V.memset(ones[:], 1.0))
                c.did(V.memset(t["ones64"][:], 1.0))
                c.did(V.memset(t["half_pow"][:], -0.5))
                c.did(V.tensor_reduce(t["own"][:], ident.rearrange("p (v d) -> p v d", v=HH), AX.X, ALU.add))
                c.did(V.memset(t["mparts"][:], 0.0))
                c.did(V.tensor_reduce(t["pick"][:], ident.rearrange("p (g h) -> p h g", h=H), AX.X, ALU.add))
                c.wait()
                c.did(V.tensor_copy(t["pick_b"][:], t["pick"][:].unsqueeze(2).to_broadcast([P, H, P])))
                c.did(V.tensor_scalar(t["bq"][:], t["bq"][:], 1.0 / HD ** 0.5, None, ALU.mult))
                c.did(V.tensor_scalar(t["gamma"][:], t["gamma"][:], 0.5, None, ALU.mult))
                c.did(V.tensor_scalar(t["beta"][:], t["beta"][:], 0.5, None, ALU.mult))
                for s in range(2):
                    c.did(V.memset(t["v1"][:, s, :, :, HD], 1.0))
                for raw_, s_, r_, ci, nch in ((rawf, su, ru, cu, 2 * FC), (rawd, sd, rd, cd, KC)):
                    flat = raw_.rearrange("p a c d -> p (a c d)") if raw_ is rawf else raw_.rearrange("p c d -> p (c d)")
                    blocks = flat.rearrange("p (n q) -> p n q", q=QBLOCK)
                    nb = blocks.shape[1]
                    c.did(V.tensor_reduce(s_[:], blocks, AX.X, ALU.max, apply_absolute_value=True))
                    c.wait()
                    c.did(V.tensor_scalar(s_[:], s_[:], 1.0 / 7.0, TINY, ALU.mult, ALU.max))
                    c.wait()
                    c.did(V.reciprocal(r_[:], s_[:]))
                    top = t["top_u"] if raw_ is rawf else cdm
                    c.did(V.tensor_reduce(top[:], s_.rearrange("p (c n) -> p c n", c=nch), AX.X, ALU.max))
                    c.wait()
                    c.did(V.reciprocal(ci[:], top[:]))
                    c.did(V.tensor_tensor(blocks, blocks, r_[:].unsqueeze(2).to_broadcast([P, nb, QBLOCK]), ALU.mult))
                    c.wait()
                    c.did(V.tensor_scalar(flat, flat, MAGIC, -MAGIC, ALU.add, ALU.add))
                    c.did(V.tensor_tensor(s_.rearrange("p (c n) -> p c n", c=nch), s_.rearrange("p (c n) -> p c n", c=nch),
                                          ci[:].unsqueeze(2).to_broadcast([P, nch, nb // nch]), ALU.mult))
                    c.wait()
                    c.did(V.tensor_tensor(blocks, blocks, s_[:].unsqueeze(2).to_broadcast([P, nb, QBLOCK]), ALU.mult))
                    c.wait()
                dve.sem_inc(quantised, 1)
                n = 0

                def bank():
                    nonlocal n
                    n += 1
                    dve.wait_ge(turned, n)
                    return tps[(n - 1) % 2]

                for i in range(4):
                    src = bank()
                    V.tensor_copy(t["w_x"][:, i].rearrange("p k o -> p (k o)"), src[:]).then_inc(taken, 1)
                for hi, lo in ([(t["w_uh"], t["w_ul"])] * (2 * FC * KC // 4) + [(t["w_dh"], t["w_dl"])] * (KC * FC // 4)):
                    src = bank()
                    g = n - 5 if hi is t["w_uh"] else n - 5 - 2 * FC * KC // 4
                    h_, l_ = hi[:, g * 512:(g + 1) * 512], lo[:, g * 512:(g + 1) * 512]
                    c.did(V.tensor_copy(h_, src[:]))
                    c.wait()
                    V.tensor_tensor(l_, src[:], h_, ALU.subtract).then_inc(taken, 1)
                dve.wait_ge(row_made, 1)
                c.did(V.tensor_copy(cdt[:], tps[0][0:1, 0:D]))
                c.wait()
                dve.sem_inc(quantised, 1)
                dve.wait_ge(row_made, 2)
                V.tensor_copy(t["top_d"][:], tps[1][:, 0:D]).then_inc(taken, 1)

            @block.tensor
            def _(pe):
                T = nc.tensor
                ident = t["ident"]
                pe.wait_ge(quantised, 1)
                n = 0

                def four(parts):
                    nonlocal n
                    if n >= 2:
                        pe.wait_ge(taken, n - 1)
                    for j, src in enumerate(parts):
                        m = T.transpose(tps[n % 2][:, j * P:(j + 1) * P], src, ident[:])
                    m.then_inc(turned, 1)
                    n += 1

                for i in range(4):
                    four([raw[:, i, oc, kc * P:(kc + 1) * P] for kc in range(KC) for oc in range(KC)])
                up = [rawf[:, a, c_, kc * P:(kc + 1) * P] for kc in range(KC) for a in range(2) for c_ in range(FC)]
                for g in range(len(up) // 4):
                    four(up[4 * g:4 * g + 4])
                dn = [rawd[:, oc, c_ * P:(c_ + 1) * P] for c_ in range(FC) for oc in range(KC)]
                for g in range(len(dn) // 4):
                    four(dn[4 * g:4 * g + 4])
                pe.wait_ge(taken, NT)
                for oc in range(KC):
                    m = T.transpose(tps[0][0:1, oc * P:(oc + 1) * P], cdm[:, oc:oc + 1], ident[:])
                m.then_inc(row_made, 1)
                pe.wait_ge(quantised, 2)
                T.matmul(tps[1][:, 0:D], ones[:], cdt[:], start=True, stop=True).then_inc(row_made, 1)


def recurrence_block(nc, t, x_d, o_d):
    DH = 5
    GH = HH - DH
    XS = 4
    STEPS = 8
    HALFSTEP = STEPS // 2
    with ExitStack() as ctx:
        def sb(name, shape, dt=F32):
            return ctx.enter_context(nc.sbuf_tensor(name, shape, dt))

        def sem(name):
            return ctx.enter_context(nc.semaphore(name))

        xin = sb("rec_x", [P, XS, D])
        xT = sb("rec_xT", [P, 2, KC, P])
        qkvg = sb("rec_qkvg", [P, 2, 4, P])
        state_v = sb("state_v", [P, DH * HD * HD])
        kv_v = sb("kv_v", [P, DH * HD * HD])
        sq_v = sb("sq_v", [P, DH * HD * HD])
        state_g = sb("state_g", [P, GH * HD * HD])
        kv_g = sb("kv_g", [P, GH * HD * HD])
        sq_g = sb("sq_g", [P, 2, GH * HD * HD])
        outb = sb("rec_out", [P, 2, HALFSTEP, P])
        tp = [ctx.enter_context(nc.psum_tensor(f"rec_tp{i}", [P, 512], F32)) for i in range(2)]
        pj = [ctx.enter_context(nc.psum_tensor(f"rec_pj{i}", [P, 512], F32)) for i in range(2)]

        x_loaded = [sem(f"x_loaded{i}") for i in range(XS)]
        x_turned = sem("x_turned")
        xT_ready = sem("xT_ready")
        projected = sem("projected")
        qkvg_ready = sem("qkvg_ready")
        v_used = sem("v_used")
        g_product = sem("g_product")
        stored = [sem(f"stored{i}") for i in range(2)]
        vchain = sem("rec_vchain")
        gchain = sem("rec_gchain")
        zeroed = sem("rec_zeroed")
        CR = 2

        o_view = o_d.rearrange("b t (h c) -> h b t c", h=HALF)

        with nc.Block() as block:

            @block.sync
            def _(sp):
                for u in range(2):
                    sp.sem_inc(stored[u], 32)

                def load(pair, slot):
                    for k in range(2):
                        sp.dma_start(xin[k * B:(k + 1) * B, slot, :], x_d[:, bass.ds(pair * 2 + k, 1), :]
                                     .rearrange("b a d -> b (a d)")).then_inc(x_loaded[slot], 16)

                def store(half, slot):
                    sp.wait_ge(v_used, CR + HALFSTEP * (half + 1))
                    for h in range(HALF):
                        sp.dma_start(o_view[h][:, bass.ds(half * HALFSTEP, HALFSTEP), :],
                                     outb[h * B:(h + 1) * B, slot]).then_inc(stored[slot], 16)

                for pair in range(XS):
                    load(pair, pair)
                NHALF = S // HALFSTEP
                with sp.Fori(0, NHALF // 2 - 1) as j:
                    for u in range(2):
                        store(2 * j + u, u)
                        for k in range(2):
                            load(4 * j + 2 * u + XS + k, (2 * u + k) % XS)
                for u in range(2):
                    store(NHALF - 2 + u, u)
                for u in range(2):
                    sp.wait_ge(stored[u], 32 + 16 * NHALF)

            @block.tensor
            def _(pe):
                T = nc.tensor
                pe.sem_inc(x_turned, CR)
                pe.sem_inc(projected, 3)
                with pe.Fori(0, S // STEPS) as i:
                    for p in range(STEPS // 2):
                        pair = i * (STEPS // 2) + p
                        pe.wait_ge(x_loaded[p % XS], 32 * (i + 1))
                        pe.wait_ge(xT_ready, pair + 1)
                        for kc in range(KC):
                            m = T.transpose(tp[p % 2][:, kc * P:(kc + 1) * P], xin[:, p % XS, kc * P:(kc + 1) * P],
                                            t["ident"][:])
                        m.then_inc(x_turned, 1)
                        pe.wait_ge(xT_ready, CR + pair + 1)
                        for k in range(2):
                            step = i * STEPS + 2 * p + k
                            pe.wait_ge(qkvg_ready, 2 * step + 2)
                            for h in range(HALF):
                                o = pj[k][h * B:(h + 1) * B, :]
                                for kc in range(KC):
                                    T.matmul(o, xT[:, p % 2, kc, k * B:(k + 1) * B],
                                             t["w_rec"][:, kc, h].rearrange("p a c -> p (a c)"),
                                             start=(kc == 0), stop=False)
                                m = T.matmul(o[:, 3 * P:], t["ones64"][:], t["bf_row"][:, h * P:(h + 1) * P],
                                             start=False, stop=True)
                            m.then_inc(projected, 1)

            @block.scalar
            def _(act):
                A = nc.scalar
                act.sem_inc(xT_ready, CR)
                act.sem_inc(qkvg_ready, 2 * CR)
                with act.Fori(0, S // STEPS) as i:
                    for p in range(STEPS // 2):
                        pair = i * (STEPS // 2) + p
                        act.wait_ge(x_turned, CR + pair + 1)
                        act.wait_ge(projected, 2 * pair + 1)
                        A.activation(xT[:, p % 2].rearrange("p k n -> p (k n)"), tp[p % 2][:, 0:KC * P],
                                     ACT.Copy).then_inc(xT_ready, 1)
                        for k in range(2):
                            step = i * STEPS + 2 * p + k
                            act.wait_ge(projected, 3 + step + 1)
                            act.wait_ge(v_used, step + 1)
                            act.wait_ge(g_product, step + 1)
                            A.activation(qkvg[:, k, 0:3].rearrange("p a c -> p (a c)"), pj[k][:, 0:3 * P],
                                         ACT.Copy).then_inc(qkvg_ready, 1)
                            A.activation(qkvg[:, k, 3], pj[k][:, 3 * P:], ACT.Sigmoid).then_inc(qkvg_ready, 1)

            def factors(slot, lo, n):
                shape = [P, n, HD, HD]
                q, k, v, g = (qkvg[:, slot, a, lo * HD:(lo + n) * HD].rearrange("p (h c) -> p h c", h=n)
                              for a in range(4))
                return (q.unsqueeze(2).to_broadcast(shape), k.unsqueeze(2).to_broadcast(shape),
                        v.unsqueeze(3).to_broadcast(shape), g.unsqueeze(3).to_broadcast(shape))

            def cube(ap, n):
                return ap.rearrange("p (h i j) -> p h i j", h=n, i=HD)

            @block.vector
            def _(dve):
                V = nc.vector
                dve.sem_inc(v_used, CR)
                V.memset(state_v[:], 0.0).then_inc(vchain, 1)
                PER = 5
                with dve.Fori(0, S // STEPS) as i:
                    for s in range(STEPS):
                        step = i * STEPS + s
                        c = Chain(dve, vchain, 1 + step * PER)
                        q, k, v, g = factors(s % 2, 0, DH)
                        dve.wait_ge(qkvg_ready, 2 * (CR + step + 1))
                        c.wait()
                        c.did(V.tensor_tensor(cube(kv_v, DH), v, k, ALU.mult))
                        c.did(V.tensor_tensor(cube(state_v, DH), cube(state_v, DH), g, ALU.mult))
                        c.wait()
                        c.did(V.tensor_tensor(state_v[:], state_v[:], kv_v[:], ALU.add))
                        c.wait()
                        c.did(V.tensor_tensor(cube(sq_v, DH), cube(state_v, DH), q, ALU.mult))
                        if s % HALFSTEP == 0:
                            dve.wait_ge(stored[s // HALFSTEP], 32 * (i + 1))
                        c.wait()
                        o = outb[:, s // HALFSTEP, s % HALFSTEP]
                        c.did(V.tensor_reduce(o[:, 0:DH * HD], sq_v.rearrange("p (n j) -> p n j", j=HD), AX.X, ALU.add))
                        assert c.n == PER
                        dve.wait_ge(g_product, CR + step + 1)
                        V.tensor_reduce(o[:, DH * HD:], sq_g[:, s % 2].rearrange("p (n j) -> p n j", j=HD),
                                        AX.X, ALU.add).then_inc(v_used, 1)

            @block.gpsimd
            def _(pool):
                G = nc.gpsimd
                pool.sem_inc(g_product, CR)
                G.memset(state_g[:], 0.0).then_inc(gchain, 1)
                PER = 3
                with pool.Fori(0, S // STEPS) as i:
                    for s in range(STEPS):
                        step = i * STEPS + s
                        c = Chain(pool, gchain, 1 + step * PER)
                        q, k, v, g = factors(s % 2, DH, GH)
                        pool.wait_ge(qkvg_ready, 2 * (CR + step + 1))
                        c.wait()
                        c.did(G.tensor_tensor(cube(kv_g, GH), v, k, ALU.mult))
                        c.did(G.tensor_tensor(cube(state_g, GH), cube(state_g, GH), g, ALU.mult))
                        c.wait()
                        c.did(G.tensor_tensor(state_g[:], state_g[:], kv_g[:], ALU.add))
                        assert c.n == PER
                        c.wait()
                        pool.wait_ge(v_used, step + 1)
                        G.tensor_tensor(cube(sq_g[:, s % 2], GH), cube(state_g, GH), q, ALU.mult).then_inc(g_product, 1)
                        pool.wait_ge(g_product, CR + step + 1)


def attention_block(nc, t, x_d, ctx_d, o_d):
    NP = B // 2
    CR = 2
    NV = 5
    with ExitStack() as ctx:
        def sb(name, shape, dt=F32):
            return ctx.enter_context(nc.sbuf_tensor(name, shape, dt))

        def sem(name):
            return ctx.enter_context(nc.semaphore(name))

        def bank(name):
            return ctx.enter_context(nc.psum_tensor(name, [P, 512], F32))

        xs = sb("att_x", [P, 2, 2, D])
        cs = sb("att_ctx", [P, 2, 2, D])
        os_ = sb("att_o", [P, 2, 2, D])
        xT = sb("att_xT", [P, KC, 2 * P])
        cT = sb("att_cT", [P, KC, 2 * P])
        on = sb("att_on", [P, 2, D])
        ogb = sb("att_ogb", [P, KC, 2 * P])
        th = sb("att_tanh", [P, KC * 2 * P])
        sg = sb("att_silu", [P, KC * 2 * P])
        yT = sb("att_yT", [P, KC, 2 * P])
        res1 = sb("att_res1", [P, 2, D])
        x1 = sb("att_x1", [P, 2, D])
        x1b = sb("att_x1b", [P, 2, 2, D])
        x1T = sb("att_x1T", [P, KC, 2 * P])
        kT = sb("att_kT", [P, 2, KC, 2 * P])
        qT = sb("att_qT", [P, KC, 2 * P])
        qm = sb("att_qm", [P, 2, KC, 2, HH, P])
        st_o = sb("st_o", [P, 2, 6])
        mv_o = sb("mv_o", [P, 2, 2])
        rs_o = sb("rs_o", [P, 2])
        st_1 = sb("st_1", [P, 2, 6])
        mv_1 = sb("mv_1", [P, 2, 2])
        rs_1 = sb("rs_1", [P, 2])
        st_2 = sb("st_2", [P, 6])
        mv_2 = sb("mv_2", [P, 2])
        rs_2 = sb("rs_2", [P, 1])
        mneg = sb("mneg", [P, H])
        mT = sb("mT", [P, P], BF16)
        e = sb("att_e", [P, 2, 512])
        rc = sb("att_rc", [P, H])
        att = sb("att_att", [P, D])
        attT = sb("att_attT", [P, KC, P])
        res2 = sb("att_res2", [P, D])

        F0, F1, F2, BA = bank("bank_f0"), bank("bank_f1"), bank("bank_f2"), bank("bank_a")
        SB = [bank("bank_s0"), bank("bank_s1")]
        TB = [bank("bank_t0"), bank("bank_t1")]
        BA16 = BA[:, 0:64].bitcast(BF16)
        BAV = BA[:, 0:H * (HD + 1)].rearrange("p (h c) -> p h c", h=H)

        a_loaded = [sem(f"a_loaded{i}") for i in range(2)]
        names = """xT_made xT_ready cT_made cT_ready zg_made th_ready on_ready onT_made ogb_ready y_ready
            zg_taken k_made k_ready v_made v_ready wout_made res1_ready x1_ready x1T_made x1T_ready q_made q_flat q_maskv q_maska
            var_o rstd_o var_1 rstd_1 x1b_ready s_made s_taken m_ready mt_made mt_ready t_made e_ready pv_made
            att_ready attT_made attT_ready wo_made res2_ready var_2 rstd_2 a_front a_attn""".split()
        q = {n: sem(n) for n in names}

        def steps(eng, step):
            step(0, 0, 0, True, False)
            with eng.Fori(0, (NP - 2) // 2) as j:
                for u in range(2):
                    step(2 * j + 1 + u, (1 + u) % 2, j + u, True, True)
            step(NP - 1, 1, (NP - 2) // 2, True, True)
            step(NP, 0, NP // 2, False, True)

        with nc.Block() as block:

            @block.sync
            def _(sp):
                def load(pair, slot):
                    rows = bass.ds(2 * pair, 2)
                    for dst, src in ((xs, x_d), (cs, ctx_d), (os_, o_d)):
                        sp.dma_start(dst[:, slot], src[rows].rearrange("b t d -> t b d")).then_inc(a_loaded[slot], 16)

                load(0, 0)
                load(1, 1)
                with sp.Fori(0, (NP - 2) // 2) as j:
                    for u in range(2):
                        sp.wait_ge(q["x1_ready"], 2 * (2 * j + 1 + u))
                        load(2 * j + 2 + u, u)

            @block.tensor
            def _(pe):
                T = nc.tensor
                ident = t["ident"]
                wx = t["w_x"]
                pe.sem_inc(q["pv_made"], CR)

                def turn4(bank_, src, done):
                    for kc in range(KC):
                        for b in range(2):
                            m = T.transpose(bank_[:, (2 * kc + b) * P:(2 * kc + b + 1) * P],
                                            src[:, b, kc * P:(kc + 1) * P], ident[:])
                    m.then_inc(done, 1)

                def across(bank_, wt, rhs, done):
                    for oc in range(KC):
                        for kc in range(KC):
                            m = T.matmul(bank_[:, oc * 2 * P:(oc + 1) * 2 * P], wt[:, kc, oc * P:(oc + 1) * P],
                                         rhs[:, kc], start=(kc == 0), stop=(kc == KC - 1))
                    m.then_inc(done, 1)

                def along(bank_, lhs, wt, done):
                    for b in range(2):
                        for kc in range(KC):
                            m = T.matmul(bank_[:, b * D:(b + 1) * D], lhs[:, kc, b * P:(b + 1) * P], wt[:, kc],
                                         start=(kc == 0), stop=(kc == KC - 1))
                    m.then_inc(done, 1)

                def scores(n, s, b):
                    for g in range(4):
                        pe.wait_ge(q["s_taken"], 4 * n + g + 1)
                        for m_ in range(4):
                            h = 4 * g + m_
                            m = T.matmul(SB[g % 2][:, m_ * P:(m_ + 1) * P], qm[:, s, h // HH, b, h % HH],
                                         kT[:, s, h // HH, b * P:(b + 1) * P], start=True, stop=True)
                        m.then_inc(q["s_made"], 1)

                def shift(n):
                    pe.wait_ge(q["m_ready"], n + 1)
                    T.transpose(BA16, t["mparts"].rearrange("p a h -> p (a h)"), t["ident_b"][:]).then_inc(q["mt_made"], 1)

                def probs_values(n, s, b):
                    pe.wait_ge(q["mt_ready"], n + 1)
                    for g in range(5):
                        if g < 4:
                            pe.wait_ge(q["e_ready"], 4 * n + g + 1)
                            kc, v = g // 2, g % 2 * 4
                            T.matmul(TB[g % 2][:], kT[:, s, kc, b * P:(b + 1) * P],
                                     qm[:, s, kc, b, v:v + 4].rearrange("p h q -> p (h q)"), start=True, stop=False)
                            for m_ in range(4):
                                m = T.matmul(TB[g % 2][:, m_ * P:(m_ + 1) * P], t["pick_b"][:, 4 * g + m_], mT[:],
                                             start=False, stop=(m_ == 3))
                            m.then_inc(q["t_made"], 1)
                        if g >= 1:
                            pe.wait_ge(q["e_ready"], CR + 4 * n + g)
                            for m_ in range(4):
                                h = 4 * (g - 1) + m_
                                m = T.matmul(BAV[:, h], e[:, (g - 1) % 2, m_ * P:(m_ + 1) * P], t["v1"][:, s, b, h],
                                             start=True, stop=True)
                            m.then_inc(q["pv_made"], 1)

                def att_turn(n):
                    pe.wait_ge(q["att_ready"], n + 1)
                    for kc in range(KC):
                        m = T.transpose(BA[:, kc * P:(kc + 1) * P], att[:, kc * P:(kc + 1) * P], ident[:])
                    m.then_inc(q["attT_made"], 1)

                def att_out(n):
                    pe.wait_ge(q["attT_ready"], n + 1)
                    for kc in range(KC):
                        m = T.matmul(BA[:, 0:D], attT[:, kc], wx[:, 3, kc], start=(kc == 0), stop=(kc == KC - 1))
                    m.then_inc(q["wo_made"], 1)

                def step(p, s, before, front, attn):
                    n0, so = 2 * p - 2, 1 - s
                    if attn:
                        pe.wait_ge(q["q_maskv"], NV * KC * p)
                        pe.wait_ge(q["q_maska"], (HH - NV) * KC * p)
                        pe.wait_ge(q["k_ready"], 2 * p)
                        scores(n0, so, 0)
                    if front:
                        pe.wait_ge(a_loaded[s], 48 * (before + 1))
                        wait_if(pe, q["x1T_ready"], p)
                        turn4(F0, xs[:, s], q["xT_made"])
                        wait_if(pe, q["q_flat"], 2 * p)
                        turn4(F1, cs[:, s], q["cT_made"])
                    if attn:
                        wait_if(pe, q["res2_ready"], n0 + 1)
                        shift(n0)
                    if front:
                        pe.wait_ge(q["xT_ready"], p + 1)
                        wait_if(pe, q["zg_taken"], p)
                        across(F2, t["w_g"], xT, q["zg_made"])
                    if attn:
                        probs_values(n0, so, 0)
                    if front:
                        pe.wait_ge(q["on_ready"], 2 * p + 2)
                        turn4(F0, on, q["onT_made"])
                    if attn:
                        scores(n0 + 1, so, 1)
                        att_turn(n0)
                    if front:
                        pe.wait_ge(q["cT_ready"], p + 1)
                        across(F1, wx[:, 1], cT, q["k_made"])
                        pe.wait_ge(q["ogb_ready"], 2 * p + 2)
                        along(F0, cT, wx[:, 2], q["v_made"])
                    if attn:
                        pe.wait_ge(q["attT_ready"], n0 + 1)
                        shift(n0 + 1)
                        pe.wait_ge(q["mt_ready"], n0 + 2)
                        att_out(n0)
                    if front:
                        pe.wait_ge(q["y_ready"], p + 1)
                        pe.wait_ge(q["k_ready"], 2 * p + 2)
                        along(F1, yT, t["w_out"], q["wout_made"])
                    if attn:
                        pe.wait_ge(q["res2_ready"], n0 + 2)
                        pe.wait_ge(q["v_ready"], p)
                        probs_values(n0 + 1, so, 1)
                    if front:
                        pe.wait_ge(q["x1_ready"], 2 * p + 2)
                        pe.wait_ge(q["v_ready"], p + 1)
                        turn4(F0, x1, q["x1T_made"])
                    if attn:
                        att_turn(n0 + 1)
                    if front:
                        pe.wait_ge(q["x1T_ready"], p + 1)
                        across(F1, wx[:, 0], x1T, q["q_made"])
                    if attn:
                        att_out(n0 + 1)

                steps(pe, step)

            @block.scalar
            def _(act):
                A = nc.scalar
                act.sem_inc(q["e_ready"], CR)

                def flat(ap):
                    return ap.rearrange("p k n -> p (k n)")

                def shift_out(n):
                    act.wait_ge(q["mt_made"], n + 1)
                    A.activation(mT[:], BA16, ACT.Copy).then_inc(q["mt_ready"], 1)

                def exps(n):
                    for g in range(4):
                        act.wait_ge(q["t_made"], 4 * n + g + 1)
                        act.wait_ge(q["pv_made"], 4 * n + g + 1)
                        A.activation(e[:, g % 2], TB[g % 2][:], ACT.Exp).then_inc(q["e_ready"], 1)

                def att_turned(n):
                    act.wait_ge(q["attT_made"], n + 1)
                    A.activation(flat(attT), BA[:, 0:D], ACT.Copy).then_inc(q["attT_ready"], 1)

                def step(p, s, before, front, attn):
                    n0 = 2 * p - 2
                    if front:
                        act.wait_ge(q["xT_made"], p + 1)
                        A.activation(flat(xT), F0[:], ACT.Copy).then_inc(q["xT_ready"], 1)
                        act.wait_ge(q["cT_made"], p + 1)
                        A.activation(flat(cT), F1[:], ACT.Copy).then_inc(q["cT_ready"], 1)
                    if attn:
                        shift_out(n0)
                    if front:
                        act.wait_ge(q["zg_made"], p + 1)
                        wait_if(act, q["zg_taken"], p)
                        A.activation(th[:], F2[:], ACT.Tanh, scale=0.5).then_inc(q["th_ready"], 1)
                    if attn:
                        exps(n0)
                    if front:
                        act.wait_ge(q["onT_made"], p + 1)
                        for kc in range(KC):
                            A.activation(ogb[:, kc], F0[:, kc * 2 * P:(kc + 1) * 2 * P], ACT.Identity,
                                         bias=t["beta"][:, kc:kc + 1], scale=t["gamma"][:, kc:kc + 1]).then_inc(q["ogb_ready"], 1)
                    if attn:
                        att_turned(n0)
                    if front:
                        act.wait_ge(q["k_made"], p + 1)
                        for kc in range(KC):
                            A.activation(kT[:, s, kc], F1[:, kc * 2 * P:(kc + 1) * 2 * P], ACT.Identity,
                                         bias=t["bk"][:, kc:kc + 1]).then_inc(q["k_ready"], 1)
                    if attn:
                        shift_out(n0 + 1)
                        exps(n0 + 1)
                    if front:
                        act.wait_ge(q["x1T_made"], p + 1)
                        A.activation(flat(x1T), F0[:], ACT.Copy).then_inc(q["x1T_ready"], 1)
                    if attn:
                        att_turned(n0 + 1)
                    if front:
                        act.wait_ge(q["q_made"], p + 1)
                        wait_if(act, q["q_maskv"], NV * KC * p)
                        for kc in range(KC):
                            A.activation(qT[:, kc], F1[:, kc * 2 * P:(kc + 1) * 2 * P], ACT.Identity,
                                         bias=t["bq"][:, kc:kc + 1], scale=1.0 / HD ** 0.5).then_inc(q["q_flat"], 1)
                        act.wait_ge(q["q_flat"], 2 * p + 2)
                        for kc in range(KC):
                            for v in range(NV, HH):
                                A.activation(qm[:, s, kc, :, v], qT[:, kc].rearrange("p (b n) -> p b n", b=2), ACT.Copy,
                                             scale=t["own"][:, v:v + 1]).then_inc(q["q_maska"], 1)

                steps(act, step)

            @block.vector
            def _(dve):
                V = nc.vector
                dve.sem_inc(q["s_taken"], CR)
                dve.sem_inc(q["res2_ready"], 1)
                KF, KA = 9, 6

                def maxima(n, c):
                    for g in range(4):
                        dve.wait_ge(q["s_made"], 4 * n + g + 1)
                        V.tensor_reduce(mneg[:, 4 * g:4 * g + 4], SB[g % 2].rearrange("p (h k) -> p h k", h=4),
                                        AX.X, ALU.max, negate=True).then_inc(q["s_taken"], 1)
                    dve.wait_ge(q["s_taken"], CR + 4 * n + 4)
                    c.did(V.tensor_copy(t["mparts"][:, 0], mneg[:]))
                    c.wait()
                    V.tensor_tensor(t["mparts"][:, 1], mneg[:], t["mparts"][:, 0], ALU.subtract).then_inc(q["m_ready"], 1)

                def softmax_norm(n, c):
                    dve.wait_ge(q["pv_made"], CR + 4 * n + 4)
                    c.did(V.reciprocal(rc[:], BAV[:, :, HD]))
                    c.wait()
                    V.tensor_tensor(att.rearrange("p (h c) -> p h c", h=H), BAV[:, :, 0:HD],
                                    rc[:].unsqueeze(2).to_broadcast([P, H, HD]), ALU.mult).then_inc(q["att_ready"], 1)

                def finish(n, s, b, c):
                    dve.wait_ge(q["wo_made"], n + 1)
                    V.tensor_tensor(res2[:], BA[:, 0:D], x1b[:, s, b], ALU.add).then_inc(q["res2_ready"], 1)
                    dve.wait_ge(q["res2_ready"], n + 2)
                    c.did(V.bn_stats(st_2[:], res2[:]))
                    c.wait_apart(t["stats_seen"])
                    c.did(V.bn_aggr(mv_2[:], st_2[:]))
                    c.wait()
                    V.tensor_scalar(mv_2[:, 1:2], mv_2[:, 1:2], EPS, None, ALU.add).then_inc(q["var_2"], 1)
                    dve.wait_ge(q["rstd_2"], n + 1)
                    x2 = t["x2"][:, bass.ds(n, 1), :].rearrange("p a d -> p (a d)")
                    c.did(V.tensor_scalar(x2, res2[:], mv_2[:, 0:1], rs_2[:], ALU.subtract, ALU.mult))
                    c.wait()
                    c.did(V.tensor_reduce(t["x2_top"][:, bass.ds(n, 1)], x2, AX.X, ALU.max, apply_absolute_value=True))

                def norm(src, st, mv, rs, var, rstd, out, ready, p, c):
                    for b in range(2):
                        c.did(V.bn_stats(st[:, b], src[:, b]))
                    c.wait_apart(t["stats_seen"])
                    for b in range(2):
                        c.did(V.bn_aggr(mv[:, b], st[:, b]))
                    c.wait()
                    V.tensor_scalar(mv[:, :, 1], mv[:, :, 1], EPS, None, ALU.add).then_inc(var, 1)
                    dve.wait_ge(rstd, p + 1)
                    for b in range(2):
                        V.tensor_scalar(out[:, b], src[:, b], mv[:, b, 0:1], rs[:, b:b + 1],
                                        ALU.subtract, ALU.mult).then_inc(ready, 1)

                def step(p, s, before, front, attn):
                    n0, so = 2 * p - 2, 1 - s
                    cf = Chain(dve, q["a_front"], KF * p)
                    ca = Chain(dve, q["a_attn"], KA * n0)
                    if attn:
                        maxima(n0, ca)
                    if front:
                        dve.wait_ge(a_loaded[s], 48 * (before + 1))
                        norm(os_[:, s], st_o, mv_o, rs_o, q["var_o"], q["rstd_o"], on, q["on_ready"], p, cf)
                    if attn:
                        softmax_norm(n0, ca)
                    if front:
                        dve.wait_ge(q["th_ready"], p + 1)
                        V.scalar_tensor_tensor(sg[:], th[:], 1.0, F2[:], ALU.add, ALU.mult).then_inc(q["zg_taken"], 1)
                        dve.wait_ge(q["zg_taken"], p + 1)
                        dve.wait_ge(q["ogb_ready"], 2 * p + 2)
                        V.tensor_tensor(yT.rearrange("p k n -> p (k n)"), sg[:], ogb.rearrange("p k n -> p (k n)"),
                                        ALU.mult).then_inc(q["y_ready"], 1)
                    if attn:
                        c1 = Chain(dve, q["a_attn"], KA * n0 + ca.n)
                        maxima(n0 + 1, c1)
                    if front:
                        dve.wait_ge(q["v_made"], p + 1)
                        for b in range(2):
                            ins = V.tensor_tensor(t["v1"][:, s, b, :, 0:HD], F0[:, b * D:(b + 1) * D].rearrange("p (h c) -> p h c", h=H),
                                                  t["bv"].rearrange("p (h c) -> p h c", h=H), ALU.add)
                            if b == 0:
                                cf.did(ins)
                        ins.then_inc(q["v_ready"], 1)
                    if attn:
                        c2 = Chain(dve, q["a_attn"], c1.start + c1.n)
                        finish(n0, so, 0, c2)
                    if front:
                        dve.wait_ge(q["wout_made"], p + 1)
                        V.tensor_tensor(res1.rearrange("p b d -> p (b d)"), xs[:, s].rearrange("p b d -> p (b d)"),
                                        F1[:], ALU.add).then_inc(q["res1_ready"], 1)
                        dve.wait_ge(q["res1_ready"], p + 1)
                        wait_if(dve, q["x1b_ready"], p)
                        norm(res1, st_1, mv_1, rs_1, q["var_1"], q["rstd_1"], x1, q["x1_ready"], p, cf)
                        assert cf.n == KF, cf.n
                    if attn:
                        c3 = Chain(dve, q["a_attn"], c2.start + c2.n)
                        softmax_norm(n0 + 1, c3)
                    if front:
                        dve.wait_ge(q["q_flat"], 2 * p + 2)
                        for kc in range(KC):
                            for v in range(NV):
                                V.tensor_scalar(qm[:, s, kc, :, v], qT[:, kc].rearrange("p (b n) -> p b n", b=2),
                                                t["own"][:, v:v + 1], None, ALU.mult).then_inc(q["q_maskv"], 1)
                    if attn:
                        dve.wait_ge(q["x1b_ready"], p)
                        finish(n0 + 1, so, 1, c3)
                        assert ca.n + c1.n + c2.n + c3.n == 2 * KA, (ca.n, c1.n, c2.n, c3.n)

                steps(dve, step)

            @block.gpsimd
            def _(pool):
                G = nc.gpsimd
                def power(var, v, mv, rs, rstd):
                    pool.wait_ge(var, v)
                    G.tensor_tensor(rs, mv, t["half_pow"][:, 0:rs.shape[1]], ALU.pow).then_inc(rstd, 1)

                def step(p, s, before, front, attn):
                    n0 = 2 * p - 2
                    if front:
                        power(q["var_o"], p + 1, mv_o[:, :, 1], rs_o[:], q["rstd_o"])
                    if attn:
                        power(q["var_2"], n0 + 1, mv_2[:, 1:2], rs_2[:], q["rstd_2"])
                    if front:
                        power(q["var_1"], p + 1, mv_1[:, :, 1], rs_1[:], q["rstd_1"])
                        pool.wait_ge(q["x1_ready"], 2 * p + 2)
                        G.tensor_tensor(x1b[:, s], x1[:], t["bo"][:].unsqueeze(1).to_broadcast([P, 2, D]),
                                        ALU.add).then_inc(q["x1b_ready"], 1)
                    if attn:
                        power(q["var_2"], n0 + 2, mv_2[:, 1:2], rs_2[:], q["rstd_2"])

                steps(pool, step)


def feedforward_block(nc, t, g_d, u_d, out_d):
    TOK = 512
    NT = B * S // TOK
    BT = TOK // S
    CR = 2
    NS = 3
    HC = FC // 2
    with ExitStack() as ctx:
        def sb(name, shape, dt=F32):
            return ctx.enter_context(nc.sbuf_tensor(name, shape, dt))

        def sem(name):
            return ctx.enter_context(nc.semaphore(name))

        top = sb("ff_top", [P, 2 * FC, NT])
        topr = sb("ff_topr", [P, 2 * FC])
        top1 = sb("ff_top1", [P, 2])
        topa = sb("ff_topa", [P, 2])
        sc = sb("ff_scales", [P, 16])
        cf = sb("ff_coef", [P, 2 * FC])
        early = ExitStack()
        xq = early.enter_context(nc.sbuf_tensor("ff_xq", [P, NT, 2, KC, TOK], F16))
        S_X, R_X, S_U, S_G, R_U, R_G, S_2, R_2, K_2, S_UO, R_O, K_O = range(12)

        def one(i):
            return sc[:, i:i + 1]

        banks = [ctx.enter_context(nc.psum_tensor(f"ff_bank{i}", [P, 512], F32)) for i in range(6)]
        turnb = [ctx.enter_context(nc.psum_tensor(f"ff_turn{i}", [P, 1024], F16)) for i in range(2)]

        def weights(part, kc, a, c):
            return t[part][:, ((kc * 2 + a) * FC + c) * P:((kc * 2 + a) * FC + c + 1) * P]

        def chunk_products(T, bank_, a, c, tile, done):
            terms = [(wp, xp, kc) for kc in range(KC) for wp, xp in (("w_uh", 0), ("w_uh", 1), ("w_ul", 0))]
            for i, (wp, xp, kc) in enumerate(terms):
                m = T.matmul(bank_[:], weights(wp, kc, a, c), tile[:, xp, kc],
                             start=(i == 0), stop=(i == len(terms) - 1))
            m.then_inc(done, 1)

        def low16(ap):
            return ap.bitcast(I16).rearrange("p (n two) -> p n two", two=2)[:, :, 0]

        with ExitStack() as c1:
            xr = c1.enter_context(nc.sbuf_tensor("s1_round", [P, 2, BT * D], F32))
            xh = c1.enter_context(nc.sbuf_tensor("s1_high", [P, 2, BT * D], F16))
            xl = c1.enter_context(nc.sbuf_tensor("s1_low", [P, 2, BT * D], F16))
            q = {n: c1.enter_context(nc.semaphore("s1_" + n)) for n in
                 "part all vchain split turned kept made maxed".split()}
            with nc.Block() as block:

                @block.vector
                def _(dve):
                    V = nc.vector
                    v = Chain(dve, q["vchain"])
                    v.did(V.tensor_reduce(top1[:, 0:1], t["x2_top"][:], AX.X, ALU.max))
                    v.wait()
                    dve.sem_inc(q["part"], 1)
                    dve.wait_ge(q["all"], 1)
                    v.did(V.tensor_scalar(one(S_X), topa[:, 0:1], 1.0 / QMAX, TINY, ALU.mult, ALU.max))
                    v.wait()
                    v.did(V.reciprocal(one(R_X), one(S_X)))
                    v.wait()
                    dve.sem_inc(q["maxed"], 6)
                    BASE = 3

                    def split(n, s, base):
                        w = Chain(dve, q["vchain"], base)
                        dve.wait_ge(q["turned"], 2 * n + 2)
                        w.did(V.tensor_scalar(xr[:, s], t["x2"][:, bass.ds(n * BT, BT), :].rearrange("p b d -> p (b d)"),
                                              one(R_X), MAGIC, ALU.mult, ALU.add))
                        w.wait()
                        w.did(V.tensor_scalar(xh[:, s], xr[:, s], MAGIC, None, ALU.subtract))
                        w.wait()
                        V.scalar_tensor_tensor(xl[:, s], xr[:, s], MAGIC, xh[:, s], ALU.subtract,
                                               ALU.subtract).then_inc(q["split"], 1)

                    def maxima(n):
                        for k in range(2 * FC):
                            dve.wait_ge(q["made"], n * 2 * FC + k + 1)
                            V.tensor_reduce(top[:, k, bass.ds(n, 1)], banks[k % 6][:], AX.X, ALU.max,
                                            apply_absolute_value=True).then_inc(q["maxed"], 1)

                    split(0, 0, BASE)
                    split(1, 1, BASE + 2)
                    with dve.Fori(0, (NT - 2) // 2) as j:
                        for u in range(2):
                            n = 2 * j + u
                            maxima(n)
                            split(n + 2, u, BASE + 4 + 4 * j + 2 * u)
                    maxima(NT - 2)
                    maxima(NT - 1)
                    dve.wait_ge(q["maxed"], 6 + NT * 2 * FC)
                    v = Chain(dve, q["vchain"], BASE + 2 * NT)
                    v.did(V.tensor_reduce(topr[:], top[:], AX.X, ALU.max))
                    v.wait()
                    v.did(V.tensor_tensor(topr[:], topr[:], t["top_u"][:], ALU.mult))
                    v.wait()
                    v.did(V.tensor_reduce(top1[:], topr.rearrange("p (a c) -> p a c", a=2), AX.X, ALU.max))
                    v.wait()
                    dve.sem_inc(q["part"], 1)
                    dve.wait_ge(q["all"], 2)
                    v.did(V.tensor_scalar(topa[:], topa[:], one(S_X), 1.0 / QMAX, ALU.mult, ALU.mult))
                    v.wait()
                    v.did(V.tensor_scalar(sc[:, S_U:S_G + 1], topa[:], TINY, None, ALU.max))
                    v.wait()
                    v.did(V.reciprocal(sc[:, R_U:R_G + 1], sc[:, S_U:S_G + 1]))
                    v.wait()
                    for a in range(2):
                        v.did(V.tensor_scalar(cf[:, a * FC:(a + 1) * FC], t["top_u"][:, a * FC:(a + 1) * FC],
                                              one(S_X), one(R_U + a), ALU.mult, ALU.mult))
                    v.wait()

                @block.gpsimd
                def _(pool):
                    pool.wait_ge(q["part"], 1)
                    nc.gpsimd.partition_all_reduce(topa[:, 0:1], top1[:, 0:1], P, RMAX).then_inc(q["all"], 1)
                    pool.wait_ge(q["part"], 2)
                    nc.gpsimd.partition_all_reduce(topa[:], top1[:], P, RMAX).then_inc(q["all"], 1)

                @block.tensor
                def _(pe):
                    T = nc.tensor
                    pe.sem_inc(q["turned"], 4)

                    def turn(n, s):
                        pe.wait_ge(q["split"], n + 1)
                        for part, src in ((0, xh), (1, xl)):
                            pe.wait_ge(q["kept"], 2 * n + part + 1)
                            for kc in range(KC):
                                for b in range(BT):
                                    m = T.transpose(turnb[part][:, (kc * BT + b) * P:(kc * BT + b + 1) * P],
                                                    src[:, s, b * D + kc * P:b * D + (kc + 1) * P], t["ident_h"][:])
                            m.then_inc(q["turned"], 1)

                    def products(n):
                        pe.wait_ge(q["kept"], 2 + 2 * n + 2)
                        tile = xq[:, bass.ds(n, 1)].rearrange("p a h k n -> p (a h) k n")
                        for k in range(2 * FC):
                            pe.wait_ge(q["maxed"], n * 2 * FC + k + 1)
                            chunk_products(T, banks[k % 6], k // FC, k % FC, tile, q["made"])

                    turn(0, 0)
                    with pe.Fori(0, NT // 2 - 1) as j:
                        for u in range(2):
                            turn(2 * j + u + 1, (u + 1) % 2)
                            products(2 * j + u)
                    turn(NT - 1, 1)
                    products(NT - 2)
                    products(NT - 1)

                @block.scalar
                def _(act):
                    act.sem_inc(q["kept"], 2)
                    with act.Fori(0, NT) as n:
                        for part in range(2):
                            act.wait_ge(q["turned"], 4 + 2 * n + part + 1)
                            nc.scalar.activation(xq[:, bass.ds(n, 1), part].rearrange("p a k n -> p (a k n)"),
                                                 turnb[part][:], ACT.Copy).then_inc(q["kept"], 1)

        def middle_sweep(name, a, scratch, pre):
            with ExitStack() as c2:
                def sb2(nm, shape, dt=F32):
                    return c2.enter_context(nc.sbuf_tensor(name + nm, shape, dt))

                r = sb2("round", [P, NS, TOK])
                rf = sb2("whole", [P, NS, TOK])
                other = sb2("other", [P, NS, TOK])
                ob = sb2("out", [P, 2, HC * TOK])
                ib = sb2("in", [P, 2, HC * TOK]) if pre else None
                q = {n_: c2.enter_context(nc.semaphore(name + n_)) for n_ in
                     "made seen rounded floated sigged ready backed chain outs maxed part all".split()}
                loaded, stored = ([c2.enter_context(nc.semaphore(f"{name}{n_}{i}")) for i in range(2)]
                                  for n_ in ("loaded", "stored"))
                with nc.Block() as block:

                    @block.tensor
                    def _(pe):
                        with pe.Fori(0, NT) as n:
                            tile = xq[:, bass.ds(n, 1)].rearrange("p a h k n -> p (a h) k n")
                            for c in range(FC):
                                pe.wait_ge(q["rounded"], n * FC + c + 1)
                                chunk_products(nc.tensor, banks[c], a, c, tile, q["made"])

                    @block.scalar
                    def _(act):
                        A = nc.scalar

                        def sigmoid(n, c):
                            act.wait_ge(q["rounded"], 6 + n * FC + c + 1)
                            act.wait_ge(q["outs"], n * FC + c + 1)
                            A.activation(other[:, c % NS], low16(r[:, c % NS]), ACT.Sigmoid,
                                         scale=one(S_G)).then_inc(q["sigged"], 1)

                        def floats(n, c):
                            act.wait_ge(q["rounded"], 6 + n * FC + c + 1)
                            act.wait_ge(q["outs"], n * FC + c + 1)
                            A.activation(rf[:, c % NS], r[:, c % NS], ACT.Copy, bias=-MAGIC).then_inc(q["floated"], 1)

                        def back(n, c):
                            act.wait_ge(q["ready"], n * FC + c + 1)
                            A.activation(other[:, c % NS], other[:, c % NS], ACT.Copy,
                                         bias=-(MAGIC if pre else MAGIC16)).then_inc(q["backed"], 1)

                        first = floats if pre else sigmoid
                        with act.Fori(0, NT) as n:
                            first(n, 0)
                            for c in range(FC):
                                if c + 1 < FC:
                                    first(n, c + 1)
                                back(n, c)

                    @block.gpsimd
                    def _(pool):
                        G = nc.gpsimd

                        def floats(n, c):
                            pool.wait_ge(q["rounded"], 6 + n * FC + c + 1)
                            pool.wait_ge(q["outs"], n * FC + c + 1)
                            pool.sem_inc(q["seen"], 1)
                            G.tensor_scalar(rf[:, c % NS], r[:, c % NS], 1.0, -MAGIC, ALU.mult,
                                            ALU.add).then_inc(q["floated"], 1)

                        with pool.Fori(0, NT) as n:
                            if not pre:
                                floats(n, 0)
                            for c in range(FC):
                                if not pre and c + 1 < FC:
                                    floats(n, c + 1)
                                if c % HC == 0:
                                    pool.wait_ge(stored[c // HC], 16 * (n + 1))
                                    pool.wait_ge(q["maxed"], n * FC + c + HC)
                                pool.wait_ge(q["floated"], n * FC + c + 1)
                                pool.wait_ge(q["backed"], n * FC + c + 1)
                                G.tensor_tensor(ob[:, c // HC, c % HC * TOK:(c % HC + 1) * TOK], other[:, c % NS],
                                                rf[:, c % NS], ALU.mult).then_inc(q["outs"], 1)
                        pool.wait_ge(q["part"], 1)
                        nc.gpsimd.partition_all_reduce(topa[:, 0:1], top1[:, 0:1], P, RMAX).then_inc(q["all"], 1)

                    @block.vector
                    def _(dve):
                        V = nc.vector
                        dve.sem_inc(q["rounded"], 6)
                        dve.sem_inc(q["outs"], NS)
                        dve.sem_inc(q["maxed"], FC)

                        def rounded(n, c):
                            dve.wait_ge(q["made"], n * FC + c + 1)
                            dve.wait_ge(q["outs"], n * FC + c + 1)
                            V.tensor_scalar(r[:, c % NS], banks[c][:], cf[:, a * FC + c:a * FC + c + 1], MAGIC,
                                            ALU.mult, ALU.add).then_inc(q["rounded"], 1)

                        def factor(n, c):
                            if pre:
                                if c % HC == 0:
                                    dve.wait_ge(loaded[c // HC], 16 * (n + 1))
                                V.tensor_scalar(other[:, c % NS], ib[:, c // HC, c % HC * TOK:(c % HC + 1) * TOK],
                                                one(K_2), MAGIC, ALU.mult, ALU.add).then_inc(q["ready"], 1)
                            else:
                                dve.wait_ge(q["sigged"], n * FC + c + 1)
                                V.tensor_scalar(other[:, c % NS], other[:, c % NS], SIG_TOP, MAGIC16,
                                                ALU.min, ALU.add).then_inc(q["ready"], 1)

                        def largest(n, c):
                            dve.wait_ge(q["outs"], NS + n * FC + c + 1)
                            V.tensor_reduce(top[:, c, bass.ds(n, 1)], ob[:, c // HC, c % HC * TOK:(c % HC + 1) * TOK],
                                            AX.X, ALU.max, apply_absolute_value=True).then_inc(q["maxed"], 1)

                        with dve.Fori(0, NT) as n:
                            for c in range(FC + 2):
                                if c < FC:
                                    rounded(n, c)
                                if 0 <= c - 1 < FC:
                                    factor(n, c - 1)
                                if c >= 2:
                                    largest(n, c - 2)
                        dve.wait_ge(q["maxed"], FC + NT * FC)
                        v = Chain(dve, q["chain"])
                        v.did(V.tensor_reduce(top1[:, 0:1], top[:, 0:FC].rearrange("p c n -> p (c n)"), AX.X, ALU.max))
                        v.wait()
                        dve.sem_inc(q["part"], 1)
                        dve.wait_ge(q["all"], 1)
                        if not pre:
                            v.did(V.tensor_scalar(topa[:, 1:2], topa[:, 0:1], one(S_G), 1.0 / QMAX, ALU.mult, ALU.mult))
                            v.wait()
                            v.did(V.tensor_scalar(one(S_2), topa[:, 1:2], TINY, None, ALU.max))
                            v.wait()
                            v.did(V.reciprocal(one(R_2), one(S_2)))
                            v.wait()
                            v.did(V.tensor_scalar(one(K_2), one(R_2), one(S_G), None, ALU.mult))
                            v.wait()
                        else:
                            v.did(V.tensor_scalar(one(K_O), one(S_U), one(S_2), None, ALU.mult))
                            v.wait()
                            v.did(V.tensor_scalar(topa[:, 1:2], topa[:, 0:1], one(K_O), 1.0 / QMAX, ALU.mult, ALU.mult))
                            v.wait()
                            v.did(V.tensor_scalar(one(S_UO), topa[:, 1:2], TINY, None, ALU.max))
                            v.wait()
                            v.did(V.reciprocal(one(R_O), one(S_UO)))
                            v.wait()
                            v.did(V.tensor_scalar(one(K_O), one(K_O), one(R_O), None, ALU.mult))
                            v.wait()

                    @block.sync
                    def _(sp):
                        for s in range(2):
                            sp.sem_inc(stored[s], 16)

                        def part(d, n, s):
                            return d[bass.ds(n, 1), :, s * HC * TOK:(s + 1) * HC * TOK].rearrange("a p n -> (a p) n")

                        def load(n, s):
                            sp.dma_start(ib[:, s], part(scratch[0], n, s)).then_inc(loaded[s], 16)

                        def store(n, s):
                            sp.wait_ge(q["outs"], NS + FC * n + HC * (s + 1))
                            sp.dma_start(part(scratch[1], n, s), ob[:, s]).then_inc(stored[s], 16)

                        if pre:
                            load(0, 0)
                            load(0, 1)
                        with sp.Fori(0, NT - 1) as n:
                            for s in range(2):
                                store(n, s)
                                if pre:
                                    load(n + 1, s)
                        store(NT - 1, 0)
                        store(NT - 1, 1)
                        for s in range(2):
                            sp.wait_ge(stored[s], 16 + 16 * NT)

        middle_sweep("s2_", 1, (None, g_d), False)
        middle_sweep("s3_", 0, (g_d, u_d), True)
        early.close()

        with ExitStack() as c4:
            def sb4(nm, shape, dt=F32):
                return c4.enter_context(nc.sbuf_tensor("s4_" + nm, shape, dt))

            W = FC * TOK
            pin = sb4("in", [P, 2, W])
            hi = sb4("high", [P, W], F16)
            lo = sb4("low", [P, W], F16)
            y = sb4("y", [P, 2, D])
            st = sb4("st", [P, 2, 6])
            mv = sb4("mv", [P, 2, 2])
            rs = sb4("rs", [P, 2])
            ob = sb4("out", [P, 2, BT, D])
            q = {n_: c4.enter_context(nc.semaphore("s4_" + n_)) for n_ in
                 "rounded high low made scaled var rstd outs chain".split()}
            loaded, stored = ([c4.enter_context(nc.semaphore(f"s4_{n_}{i}")) for i in range(2)]
                              for n_ in ("loaded", "stored"))
            with nc.Block() as block:

                @block.sync
                def _(sp):
                    for s in range(2):
                        sp.sem_inc(stored[s], 16)

                    def load(n, s):
                        sp.dma_start(pin[:, s], u_d[bass.ds(n, 1)].rearrange("a p n -> (a p) n")).then_inc(loaded[s], 16)

                    def store(n, s):
                        sp.wait_ge(q["outs"], BT * (n + 1))
                        sp.dma_start(out_d[bass.ds(n * BT, BT)].rearrange("b t d -> t b d"), ob[:, s]).then_inc(stored[s], 16)

                    load(0, 0)
                    load(1, 1)
                    with sp.Fori(0, NT // 2 - 1) as j:
                        for u in range(2):
                            sp.wait_ge(q["low"], 2 * j + u + 1)
                            load(2 * j + u + 2, u)
                            store(2 * j + u, u)
                    store(NT - 2, 0)
                    store(NT - 1, 1)
                    for s in range(2):
                        sp.wait_ge(stored[s], 16 + 8 * NT)

                @block.scalar
                def _(act):
                    with act.Fori(0, NT // 2) as j:
                        for u in range(2):
                            n = 2 * j + u
                            act.wait_ge(q["rounded"], n + 1)
                            act.wait_ge(q["made"], n * BT + 1)
                            nc.scalar.activation(hi[:], pin[:, u], ACT.Copy, bias=-MAGIC).then_inc(q["high"], 1)

                @block.tensor
                def _(pe):
                    T = nc.tensor
                    pe.sem_inc(q["made"], 1)
                    with pe.Fori(0, NT) as n:
                        pe.wait_ge(q["low"], n + 1)
                        for b in range(BT):
                            pe.wait_ge(q["scaled"], n * BT + b + 1)
                            i = 0
                            for c in range(FC):
                                at = slice(c * TOK + b * S, c * TOK + (b + 1) * S)
                                for xp, wp in ((hi, "w_dh"), (hi, "w_dl"), (lo, "w_dh")):
                                    m = T.matmul(banks[b][:, 0:D], xp[:, at], t[wp][:, c * D:(c + 1) * D],
                                                 start=(i == 0), stop=(i == 3 * FC - 1))
                                    i += 1
                            m.then_inc(q["made"], 1)

                @block.gpsimd
                def _(pool):
                    with pool.Fori(0, NT * BT // 2) as j:
                        for s in range(2):
                            pool.wait_ge(q["var"], 2 * j + s + 1)
                            nc.gpsimd.tensor_tensor(rs[:, s:s + 1], mv[:, s, 1:2], t["half_pow"][:, 0:1],
                                                    ALU.pow).then_inc(q["rstd"], 1)

                @block.vector
                def _(dve):
                    V = nc.vector
                    dve.sem_inc(q["scaled"], 4)
                    PER = 3
                    with dve.Fori(0, NT // 2) as j:
                        for u in range(2):
                            n = 2 * j + u
                            dve.wait_ge(loaded[u], 16 * (j + 1))
                            V.tensor_scalar(pin[:, u], pin[:, u], one(K_O), MAGIC, ALU.mult, ALU.add).then_inc(q["rounded"], 1)
                            dve.wait_ge(q["high"], n + 1)
                            V.scalar_tensor_tensor(lo[:], pin[:, u], MAGIC, hi[:], ALU.subtract,
                                                   ALU.subtract).then_inc(q["low"], 1)
                            dve.wait_ge(stored[u], 16 * (j + 1))
                            for b in range(BT):
                                k = n * BT + b
                                s = b % 2
                                c = Chain(dve, q["chain"], k * PER)
                                dve.wait_ge(q["made"], 1 + k + 1)
                                V.tensor_tensor(y[:, s], banks[b][:, 0:D], t["top_d"][:], ALU.mult).then_inc(q["scaled"], 1)
                                dve.wait_ge(q["scaled"], 4 + k + 1)
                                c.did(V.scalar_tensor_tensor(y[:, s], y[:, s], one(S_UO),
                                                             t["x2"][:, bass.ds(k, 1), :].rearrange("p a d -> p (a d)"),
                                                             ALU.mult, ALU.add))
                                c.wait()
                                c.did(V.bn_stats(st[:, s], y[:, s]))
                                c.wait_apart(t["stats_seen"])
                                c.did(V.bn_aggr(mv[:, s], st[:, s]))
                                c.wait()
                                V.tensor_scalar(mv[:, s, 1:2], mv[:, s, 1:2], EPS, None, ALU.add).then_inc(q["var"], 1)
                                dve.wait_ge(q["rstd"], k + 1)
                                V.tensor_scalar(ob[:, u, b], y[:, s], mv[:, s, 0:1], rs[:, s:s + 1], ALU.subtract,
                                                ALU.mult).then_inc(q["outs"], 1)


def decoder_layer(nc, x_d, ctx_d, w, out_d):
    with ExitStack() as ctx:
        def sb(name, shape, dt=F32):
            return ctx.enter_context(nc.sbuf_tensor(name, shape, dt))

        NT = B * S // 512
        stats_seen = ctx.enter_context(nc.semaphore("stats_seen"))
        o_d = nc.dram_tensor("rec_scratch", (B, S, D), F32).ap()
        g_d = nc.dram_tensor("gate_scratch", (NT, P, FC * 512), F32).ap()
        u_d = nc.dram_tensor("product_scratch", (NT, P, FC * 512), F32).ap()
        t = {
            "ident": sb("ident", [P, P]), "ident_b": sb("ident_b", [P, P], BF16), "ident_h": sb("ident_h", [P, P], F16),
            "half_pow": sb("half_pow", [P, 2]), "stats_seen": stats_seen,
            "w_uh": sb("w_uh", [P, KC * 2 * FC * P], F16), "w_ul": sb("w_ul", [P, KC * 2 * FC * P], F16),
            "w_dh": sb("w_dh", [P, FC * D], F16), "w_dl": sb("w_dl", [P, FC * D], F16),
            "top_u": sb("top_u", [P, 2 * FC]), "top_d": sb("top_d", [P, D]),
            "x2": sb("x2", [P, B, D]), "x2_top": sb("x2_top", [P, B]),
        }
        with ExitStack() as early:
            def se(name, shape, dt=F32):
                return early.enter_context(nc.sbuf_tensor(name, shape, dt))

            t.update({
                "own": se("own", [P, HH]), "mparts": se("mparts", [P, P // H, H], BF16), "pick": se("pick", [P, H]), "pick_b": se("pick_b", [P, H, P], BF16),
                "ones64": se("ones64", [1, B]),
                "w_rec": se("w_rec", [P, KC, HALF, 4, P]),
                "bf_row": se("bf_row", [1, D]),
                "w_g": se("w_g", [P, KC, D]), "w_out": se("w_out", [P, KC, D]),
                "w_x": se("w_x", [P, 4, KC, D]),
                "gamma": se("gamma", [P, KC]), "beta": se("beta", [P, KC]),
                "bq": se("bq", [P, KC]), "bk": se("bk", [P, KC]),
                "bv": se("bv", [P, D]), "bo": se("bo", [P, D]),
                "v1": se("v1", [P, 2, 2, H, HD + 1]),
            })
            setup_block(nc, t, w)
            recurrence_block(nc, t, x_d, o_d)
            attention_block(nc, t, x_d, ctx_d, o_d)
        feedforward_block(nc, t, g_d, u_d, out_d)


NAMES = {
    "q": "L0_attn_Wq", "k": "L0_attn_Wk", "v": "L0_attn_Wv", "f": "L0_attn_Wf", "bf": "L0_attn_bf",
    "g": "L0_attn_Wg", "out": "L0_attn_Wout", "gamma": "L0_attn_gamma", "beta": "L0_attn_beta",
    "xq": "L0_xattn_Wq", "bq": "L0_xattn_bq", "xk": "L0_xattn_Wk", "bk": "L0_xattn_bk",
    "xv": "L0_xattn_Wv", "bv": "L0_xattn_bv", "xo": "L0_xattn_Wo", "bo": "L0_xattn_bo",
    "gate": "L0_ffn_w_gate", "up": "L0_ffn_w_up", "down": "L0_ffn_w_down",
}


def kernel(**inputs):
    import numpy as np
    import concourse.bacc as bacc
    from concourse.bass_utils import run_bass_kernel_spmd as run

    nc = bacc.Bacc("TRN2", target_bir_lowering=False, num_devices=1)
    arrays, aps = {}, {}
    for short, name in {"x": "x", "ctx": "ctx_1024", **NAMES}.items():
        a = np.ascontiguousarray(inputs[name])
        arrays[f"in_{short}"] = a
        aps[short] = nc.dram_tensor(f"in_{short}", a.shape, mybir.dt.from_np(a.dtype), kind="ExternalInput").ap()
    out = nc.dram_tensor("out_0", (B, S, D), F32, kind="ExternalOutput").ap()
    decoder_layer(nc, aps["x"], aps["ctx"], aps, out)
    r = run(nc, [arrays], core_ids=[0])
    return r.results[0]["out_0"]
```

```python
from contextlib import ExitStack

import concourse.bass as bass
from concourse import mybir

ALU = mybir.AluOpType
ACT = mybir.ActivationFunctionType
AX = mybir.AxisListType
F32 = mybir.dt.float32
F16 = mybir.dt.float16
BF16 = mybir.dt.bfloat16
I16 = mybir.dt.int16
RMAX = bass.bass_isa.ReduceOp.max

P = 128
B, S, D = 64, 128, 256
H, HD = 16, 16
KC = D // P
HALF = 2
HH = H // HALF
FF = 768
FC = FF // P
QBLOCK = 32
EPS = 1e-5
MAGIC = 12582912.0
MAGIC16 = 192.0
QMAX = 32767.0
TINY = 1e-12
SIG_TOP = 65535.0 / 65536.0


class Chain:

    def __init__(self, eng, sem, start=0):
        self.eng, self.sem, self.start, self.n = eng, sem, start, 0

    def did(self, ins):
        ins.then_inc(self.sem, 1)
        self.n += 1

    def wait(self):
        self.eng.wait_ge(self.sem, self.start + self.n)

    def wait_apart(self, seen):
        self.wait()
        self.eng.sem_inc(seen, 1)


def wait_if(eng, sem, value):
    if not (isinstance(value, int) and value <= 0):
        eng.wait_ge(sem, value)


def setup_block(nc, t, w):
    with ExitStack() as ctx:
        def sb(name, shape, dt=F32):
            return ctx.enter_context(nc.sbuf_tensor(name, shape, dt))

        def sem(name):
            return ctx.enter_context(nc.semaphore(name))

        XW = ["xq", "xk", "xv", "xo"]
        raw = sb("raw_xattn", [P, 4, KC, D])
        rawf = sb("raw_ff", [P, 2, FC, D])
        rawd = sb("raw_down", [P, KC, FF])
        NB_U, NB_D = D // QBLOCK, FF // QBLOCK
        su = sb("scale_u", [P, 2 * FC * NB_U])
        ru = sb("rscale_u", [P, 2 * FC * NB_U])
        sd = sb("scale_d", [P, KC * NB_D])
        rd = sb("rscale_d", [P, KC * NB_D])
        cu = sb("rowmax_u_inv", [P, 2 * FC])
        cd = sb("rowmax_d_inv", [P, KC])
        cdm = sb("rowmax_d", [P, KC])
        cdt = sb("rowmax_d_row", [1, D])
        ones = sb("ones_row", [1, P])
        tps = [ctx.enter_context(nc.psum_tensor(f"setup_ps{i}", [P, 512], F32)) for i in range(2)]

        loaded = sem("setup_loaded")
        ident_set = sem("ident_set")
        vec = sem("setup_vec")
        quantised = sem("setup_quantised")
        turned = sem("setup_turned")
        taken = sem("setup_taken")
        row_made = sem("setup_row_made")

        NT = 16 // 4 + 2 * FC * KC // 4 + KC * FC // 4
        with nc.Block() as block:

            @block.sync
            def _(sp):
                for i, name in enumerate(XW):
                    sp.dma_start(raw[:, i], w[name].rearrange("(c p) d -> p c d", p=P)).then_inc(loaded, 16)
                sp.dma_start(rawf[:, 0], w["up"].rearrange("(c p) d -> p c d", p=P)).then_inc(loaded, 16)
                sp.dma_start(rawf[:, 1], w["gate"].rearrange("(c p) d -> p c d", p=P)).then_inc(loaded, 16)
                sp.dma_start(rawd[:], w["down"].rearrange("(c p) d -> p c d", p=P)).then_inc(loaded, 16)
                for kc in range(KC):
                    rows = slice(kc * P, (kc + 1) * P)
                    for i, name in enumerate(["q", "k", "v", "f"]):
                        sp.dma_start(t["w_rec"][:, kc, :, i, :],
                                     w[name][rows].rearrange("p (h c) -> p h c", h=HALF)).then_inc(loaded, 16)
                    sp.dma_start(t["w_g"][:, kc, :], w["g"][rows]).then_inc(loaded, 16)
                    sp.dma_start(t["w_out"][:, kc, :], w["out"][rows]).then_inc(loaded, 16)
                sp.dma_start(t["bf_row"][:], w["bf"].rearrange("(a d) -> a d", a=1)).then_inc(loaded, 16)
                for dst, src in (("gamma", "gamma"), ("beta", "beta"), ("bq", "bq"), ("bk", "bk")):
                    sp.dma_start(t[dst][:], w[src].rearrange("(c p) -> p c", p=P), allow_slow_non_contiguous=True).then_inc(loaded, 16)
                for dst in ("bv", "bo"):
                    sp.dma_start(t[dst][:], w[dst].partition_broadcast(P)).then_inc(loaded, 16)
                sp.wait_ge(loaded, 16 * 26)

            @block.gpsimd
            def _(pool):
                nc.gpsimd.memset(t["ident"][:], 0.0).then_inc(ident_set, 1)
                pool.wait_ge(ident_set, 1)
                nc.gpsimd.affine_select(out=t["ident"][:], in_=t["ident"][:], compare_op=ALU.not_equal, fill=1.0,
                                        base=0, pattern=[[-1, P]], channel_multiplier=1).then_inc(ident_set, 1)

            @block.vector
            def _(dve):
                V = nc.vector
                c = Chain(dve, vec)
                dve.wait_ge(ident_set, 2)
                dve.wait_ge(loaded, 16 * 26)
                ident = t["ident"]
                c.did(V.tensor_copy(t["ident_b"][:], ident[:]))
                c.did(V.tensor_copy(t["ident_h"][:], ident[:]))
                c.did(V.memset(ones[:], 1.0))
                c.did(V.memset(t["ones64"][:], 1.0))
                c.did(V.memset(t["half_pow"][:], -0.5))
                c.did(V.tensor_reduce(t["own"][:], ident.rearrange("p (v d) -> p v d", v=HH), AX.X, ALU.add))
                c.did(V.memset(t["mparts"][:], 0.0))
                c.did(V.tensor_reduce(t["pick"][:], ident.rearrange("p (g h) -> p h g", h=H), AX.X, ALU.add))
                c.wait()
                c.did(V.tensor_copy(t["pick_b"][:], t["pick"][:].unsqueeze(2).to_broadcast([P, H, P])))
                c.did(V.tensor_scalar(t["bq"][:], t["bq"][:], 1.0 / HD ** 0.5, None, ALU.mult))
                c.did(V.tensor_scalar(t["gamma"][:], t["gamma"][:], 0.5, None, ALU.mult))
                c.did(V.tensor_scalar(t["beta"][:], t["beta"][:], 0.5, None, ALU.mult))
                for s in range(2):
                    c.did(V.memset(t["v1"][:, s, :, :, HD], 1.0))
                for raw_, s_, r_, ci, nch in ((rawf, su, ru, cu, 2 * FC), (rawd, sd, rd, cd, KC)):
                    flat = raw_.rearrange("p a c d -> p (a c d)") if raw_ is rawf else raw_.rearrange("p c d -> p (c d)")
                    blocks = flat.rearrange("p (n q) -> p n q", q=QBLOCK)
                    nb = blocks.shape[1]
                    c.did(V.tensor_reduce(s_[:], blocks, AX.X, ALU.max, apply_absolute_value=True))
                    c.wait()
                    c.did(V.tensor_scalar(s_[:], s_[:], 1.0 / 7.0, TINY, ALU.mult, ALU.max))
                    c.wait()
                    c.did(V.reciprocal(r_[:], s_[:]))
                    top = t["top_u"] if raw_ is rawf else cdm
                    c.did(V.tensor_reduce(top[:], s_.rearrange("p (c n) -> p c n", c=nch), AX.X, ALU.max))
                    c.wait()
                    c.did(V.reciprocal(ci[:], top[:]))
                    c.did(V.tensor_tensor(blocks, blocks, r_[:].unsqueeze(2).to_broadcast([P, nb, QBLOCK]), ALU.mult))
                    c.wait()
                    c.did(V.tensor_scalar(flat, flat, MAGIC, -MAGIC, ALU.add, ALU.add))
                    c.did(V.tensor_tensor(s_.rearrange("p (c n) -> p c n", c=nch), s_.rearrange("p (c n) -> p c n", c=nch),
                                          ci[:].unsqueeze(2).to_broadcast([P, nch, nb // nch]), ALU.mult))
                    c.wait()
                    c.did(V.tensor_tensor(blocks, blocks, s_[:].unsqueeze(2).to_broadcast([P, nb, QBLOCK]), ALU.mult))
                    c.wait()
                dve.sem_inc(quantised, 1)
                n = 0

                def bank():
                    nonlocal n
                    n += 1
                    dve.wait_ge(turned, n)
                    return tps[(n - 1) % 2]

                for i in range(4):
                    src = bank()
                    V.tensor_copy(t["w_x"][:, i].rearrange("p k o -> p (k o)"), src[:]).then_inc(taken, 1)
                for hi, lo in ([(t["w_uh"], t["w_ul"])] * (2 * FC * KC // 4) + [(t["w_dh"], t["w_dl"])] * (KC * FC // 4)):
                    src = bank()
                    g = n - 5 if hi is t["w_uh"] else n - 5 - 2 * FC * KC // 4
                    h_, l_ = hi[:, g * 512:(g + 1) * 512], lo[:, g * 512:(g + 1) * 512]
                    c.did(V.tensor_copy(h_, src[:]))
                    c.wait()
                    V.tensor_tensor(l_, src[:], h_, ALU.subtract).then_inc(taken, 1)
                dve.wait_ge(row_made, 1)
                c.did(V.tensor_copy(cdt[:], tps[0][0:1, 0:D]))
                c.wait()
                dve.sem_inc(quantised, 1)
                dve.wait_ge(row_made, 2)
                V.tensor_copy(t["top_d"][:], tps[1][:, 0:D]).then_inc(taken, 1)

            @block.tensor
            def _(pe):
                T = nc.tensor
                ident = t["ident"]
                pe.wait_ge(quantised, 1)
                n = 0

                def four(parts):
                    nonlocal n
                    if n >= 2:
                        pe.wait_ge(taken, n - 1)
                    for j, src in enumerate(parts):
                        m = T.transpose(tps[n % 2][:, j * P:(j + 1) * P], src, ident[:])
                    m.then_inc(turned, 1)
                    n += 1

                for i in range(4):
                    four([raw[:, i, oc, kc * P:(kc + 1) * P] for kc in range(KC) for oc in range(KC)])
                up = [rawf[:, a, c_, kc * P:(kc + 1) * P] for kc in range(KC) for a in range(2) for c_ in range(FC)]
                for g in range(len(up) // 4):
                    four(up[4 * g:4 * g + 4])
                dn = [rawd[:, oc, c_ * P:(c_ + 1) * P] for c_ in range(FC) for oc in range(KC)]
                for g in range(len(dn) // 4):
                    four(dn[4 * g:4 * g + 4])
                pe.wait_ge(taken, NT)
                for oc in range(KC):
                    m = T.transpose(tps[0][0:1, oc * P:(oc + 1) * P], cdm[:, oc:oc + 1], ident[:])
                m.then_inc(row_made, 1)
                pe.wait_ge(quantised, 2)
                T.matmul(tps[1][:, 0:D], ones[:], cdt[:], start=True, stop=True).then_inc(row_made, 1)


def recurrence_block(nc, t, x_d, o_d):
    T = 8
    NB = S // T
    XS = 4
    R = 4
    KV_POOL = (5,)
    KV_VECTOR = [h for h in range(HH) if h not in KV_POOL]
    NPJ = 4
    IJ = HD * HD
    KEPT = HH - 1
    with ExitStack() as ctx:
        def sb(name, shape, dt=F32):
            return ctx.enter_context(nc.sbuf_tensor(name, shape, dt))

        def sem(name):
            return ctx.enter_context(nc.semaphore(name))

        xin = sb("rec_x", [P, XS, D])
        xT = sb("rec_xT", [P, 2, KC, P])
        qkv = sb("rec_qkv", [P, 2, T, 3, P])
        gate = sb("rec_gate", [P, 2, T + 1, P])
        last = sb("rec_last", [P, IJ * (T + 1)])
        spread = sb("rec_spread", [P, 2, IJ * (T + 1)])
        outb = sb("rec_out", [P, 2, T, P])
        tp = [ctx.enter_context(nc.psum_tensor(f"rec_tp{i}", [P, 512], F32)) for i in range(2)]
        pj = [ctx.enter_context(nc.psum_tensor(f"rec_pj{i}", [P, 512], F32)) for i in range(NPJ)]

        x_loaded = [sem(f"x_loaded{i}") for i in range(XS)]
        x_turned = sem("x_turned")
        xT_ready = sem("xT_ready")
        projected = sem("projected")
        qkvg_ready = sem("qkvg_ready")
        kv_v = sem("kv_v")
        kv_g = sem("kv_g")
        scanned = sem("scanned")
        gates_spread = sem("gates_spread")
        carried = sem("carried")
        sq_made = sem("sq_made")
        summed = sem("summed")
        stored = [sem(f"stored{i}") for i in range(2)]
        zeroed = sem("rec_zeroed")
        CR = 2

        o_view = o_d.rearrange("b t (h c) -> h b t c", h=HALF)
        x2_flat = t["x2"].rearrange("p b d -> p (b d)")

        def states_row(h):
            return x2_flat[:, h * IJ * (T + 1):(h + 1) * IJ * (T + 1)] if h < KEPT else last[:]

        def states(h):
            return states_row(h).rearrange("p (i j t) -> p i j t", i=HD, j=HD)

        def over(ap, h, axis, n):
            ap = ap[:, :, h * HD:(h + 1) * HD].rearrange("p t c -> p c t")
            return ap.unsqueeze(axis).to_broadcast([P, HD, HD, n])

        def product_kv(eng, engine, i, slot, h, done):
            eng.wait_ge(summed, HH * i + h + 1)
            eng.wait_ge(carried, HH * i + h + 1)
            eng.wait_ge(qkvg_ready, 2 * (NPJ + T * i + T))
            engine.tensor_tensor(states(h)[:, :, :, 1:], over(qkv[:, slot, :, 2], h, 2, T), over(qkv[:, slot, :, 1], h, 1, T),
                                 ALU.mult).then_inc(done, 1)

        with nc.Block() as block:

            @block.sync
            def _(sp):
                for u in range(2):
                    sp.sem_inc(stored[u], 32)

                def load(pair, slot):
                    for k in range(2):
                        sp.dma_start(xin[k * B:(k + 1) * B, slot, :], x_d[:, bass.ds(pair * 2 + k, 1), :]
                                     .rearrange("b a d -> b (a d)")).then_inc(x_loaded[slot], 16)

                def store(i, slot):
                    sp.wait_ge(summed, HH + HH * (i + 1))
                    for h in range(HALF):
                        sp.dma_start(o_view[h][:, bass.ds(i * T, T), :],
                                     outb[h * B:(h + 1) * B, slot]).then_inc(stored[slot], 16)

                def load_block(i):
                    for p in range(XS):
                        sp.wait_ge(x_turned, CR + XS * (i - 1) + p + 1)
                        load(XS * i + p, p)

                for pair in range(XS):
                    load(pair, pair)
                load_block(1)
                with sp.Fori(0, NB // 2 - 1) as j:
                    for u in range(2):
                        load_block(2 * j + u + 2)
                        store(2 * j + u, u)
                store(NB - 2, 0)
                store(NB - 1, 1)
                for u in range(2):
                    sp.wait_ge(stored[u], 32 + 16 * NB)

            @block.tensor
            def _(pe):
                E = nc.tensor
                pe.sem_inc(x_turned, CR)
                pe.sem_inc(projected, 3)
                with pe.Fori(0, NB) as i:
                    for p in range(T // 2):
                        pair = i * (T // 2) + p
                        pe.wait_ge(x_loaded[p % XS], 32 * (i + 1))
                        pe.wait_ge(xT_ready, pair + 1)
                        for kc in range(KC):
                            m = E.transpose(tp[p % 2][:, kc * P:(kc + 1) * P], xin[:, p % XS, kc * P:(kc + 1) * P],
                                            t["ident"][:])
                        m.then_inc(x_turned, 1)
                        pe.wait_ge(xT_ready, CR + pair + 1)
                        for k in range(2):
                            step = i * T + 2 * p + k
                            pe.wait_ge(qkvg_ready, 2 * step + 2)
                            for h in range(HALF):
                                o = pj[(2 * p + k) % NPJ][h * B:(h + 1) * B, :]
                                for kc in range(KC):
                                    E.matmul(o, xT[:, p % 2, kc, k * B:(k + 1) * B],
                                             t["w_rec"][:, kc, h].rearrange("p a c -> p (a c)"),
                                             start=(kc == 0), stop=False)
                                m = E.matmul(o[:, 3 * P:], t["ones64"][:], t["bf_row"][:, h * P:(h + 1) * P],
                                             start=False, stop=True)
                            m.then_inc(projected, 1)

            @block.scalar
            def _(act):
                A = nc.scalar
                act.sem_inc(xT_ready, CR)
                act.sem_inc(qkvg_ready, 2 * NPJ)

                def turn_out(i, p):
                    pair = i * (T // 2) + p
                    act.wait_ge(x_turned, CR + pair + 1)
                    act.wait_ge(projected, 2 * pair + 1)
                    A.activation(xT[:, p % 2].rearrange("p k n -> p (k n)"), tp[p % 2][:, 0:KC * P],
                                 ACT.Copy).then_inc(xT_ready, 1)

                def project_out(i, slot, p):
                    for s in (2 * p, 2 * p + 1):
                        act.wait_ge(projected, 3 + T * i + s + 1)
                        A.activation(qkv[:, slot, s].rearrange("p a c -> p (a c)"), pj[s % NPJ][:, 0:3 * P],
                                     ACT.Copy).then_inc(qkvg_ready, 1)
                        A.activation(gate[:, slot, 1 + s], pj[s % NPJ][:, 3 * P:], ACT.Sigmoid).then_inc(qkvg_ready, 1)

                def carry(i, h):
                    act.wait_ge(scanned, HH + HH * i + h + 1)
                    A.activation(states(h)[:, :, :, 0], states(h)[:, :, :, T], ACT.Copy).then_inc(carried, 1)

                def spread_gates(i, slot, h):
                    act.wait_ge(qkvg_ready, 2 * (NPJ + T * i + T))
                    act.wait_ge(scanned, HH * i + HH + h - 1)
                    A.activation(spread[:, h % 2].rearrange("p (i j t) -> p i j t", i=HD, j=HD),
                                 over(gate[:, slot], h, 2, T + 1), ACT.Copy).then_inc(gates_spread, 1)

                def ahead(i, slot):
                    for h in range(HH):
                        if h < 2:
                            turn_out(i + 1, h)
                        if h == 3:
                            act.wait_ge(summed, HH * i + HH)
                        if 3 <= h < 3 + T // 2:
                            project_out(i + 1, 1 - slot, h - 3)
                        if h in (3, 4):
                            turn_out(i + 1, h - 1)
                        if h < HH - 1:
                            spread_gates(i, slot, h + 1)
                        else:
                            spread_gates(i + 1, 1 - slot, 0)
                        carry(i, h)

                act.wait_ge(zeroed, 3)
                act.sem_inc(carried, HH)
                turn_out(0, 0)
                turn_out(0, 1)
                for p in range(T // 2):
                    project_out(0, 0, p)
                    if p + 2 < T // 2:
                        turn_out(0, p + 2)
                spread_gates(0, 0, 0)
                with act.Fori(0, NB // 2 - 1) as j:
                    for u in range(2):
                        ahead(2 * j + u, u)
                ahead(NB - 2, 0)
                for h in range(HH):
                    if h < HH - 1:
                        spread_gates(NB - 1, 1, h + 1)
                    carry(NB - 1, h)

            @block.vector
            def _(dve):
                V = nc.vector
                dve.sem_inc(summed, HH)
                dve.sem_inc(scanned, HH)

                def kv(j, r, h):
                    if h in KV_VECTOR:
                        product_kv(dve, V, R * j + r, r % 2, h, kv_v)

                def scan(j, r, h):
                    i = R * j + r
                    if h in KV_VECTOR:
                        dve.wait_ge(kv_v, len(KV_VECTOR) * i + KV_VECTOR.index(h) + 1)
                    else:
                        dve.wait_ge(kv_g, len(KV_POOL) * i + KV_POOL.index(h) + 1)
                    dve.wait_ge(carried, HH * i + h + 1)
                    dve.wait_ge(gates_spread, HH * i + h + 1)
                    V.tensor_tensor_scan(states_row(h), spread[:, h % 2], states_row(h), 0.0,
                                         ALU.mult, ALU.add).then_inc(scanned, 1)

                def total(j, r, h):
                    dve.wait_ge(sq_made, HH * (R * j + r) + h + 1)
                    if h == 0:
                        dve.wait_ge(stored[r % 2], 32 * (R // 2 * j + r // 2 + 1))
                    V.tensor_reduce(outb[:, r % 2, :, h * HD:(h + 1) * HD].rearrange("p t c -> p c t"),
                                    states(h)[:, :, :, 1:].rearrange("p i j t -> p i t j"),
                                    AX.X, ALU.add).then_inc(summed, 1)

                with dve.Fori(0, NB // R) as j:
                    for n in range(R * HH + 4):
                        for stage, late in ((scan, 1), (kv, 0), (total, 4)):
                            if 0 <= n - late < R * HH:
                                stage(j, (n - late) // HH, (n - late) % HH)

            @block.gpsimd
            def _(pool):
                G = nc.gpsimd
                G.memset(gate[:, :, 0], 0.0).then_inc(zeroed, 1)
                G.memset(x2_flat[:, 0:KEPT * IJ * (T + 1)].rearrange("p (n t) -> p n t", t=T + 1)[:, :, 0], 0.0).then_inc(zeroed, 1)
                G.memset(last.rearrange("p (n t) -> p n t", t=T + 1)[:, :, 0], 0.0).then_inc(zeroed, 1)
                with pool.Fori(0, NB // R) as j:
                    for r in range(R):
                        i = R * j + r
                        for h in range(HH):
                            if h + 2 in KV_POOL:
                                product_kv(pool, G, i, r % 2, h + 2, kv_g)
                            pool.wait_ge(carried, HH + HH * i + h + 1)
                            G.tensor_tensor(states(h)[:, :, :, 1:], states(h)[:, :, :, 1:], over(qkv[:, r % 2, :, 0], h, 1, T),
                                            ALU.mult).then_inc(sq_made, 1)


def attention_block(nc, t, x_d, ctx_d, o_d):
    NP = B // 2
    CR = 2
    NV, NG = 4, 2
    with ExitStack() as ctx:
        def sb(name, shape, dt=F32):
            return ctx.enter_context(nc.sbuf_tensor(name, shape, dt))

        def sem(name):
            return ctx.enter_context(nc.semaphore(name))

        def bank(name):
            return ctx.enter_context(nc.psum_tensor(name, [P, 512], F32))

        xs = sb("att_x", [P, 2, 2, D])
        cs = sb("att_ctx", [P, 2, 2, D])
        os_ = sb("att_o", [P, 2, 2, D])
        xT = sb("att_xT", [P, KC, 2 * P])
        cT = sb("att_cT", [P, KC, 2 * P])
        on = sb("att_on", [P, 2, D])
        ogb = sb("att_ogb", [P, KC, 2 * P])
        th = sb("att_tanh", [P, KC * 2 * P])
        sg = sb("att_silu", [P, KC * 2 * P])
        yT = sb("att_yT", [P, KC, 2 * P])
        res1 = sb("att_res1", [P, 2, D])
        x1 = sb("att_x1", [P, 2, D])
        x1b = sb("att_x1b", [P, 2, 2, D])
        x1T = sb("att_x1T", [P, KC, 2 * P])
        kT = sb("att_kT", [P, 2, KC, 2 * P])
        qT = sb("att_qT", [P, KC, 2 * P])
        qm = sb("att_qm", [P, 2, KC, 2, HH, P])
        st_o = sb("st_o", [P, 2, 6])
        mv_o = sb("mv_o", [P, 2, 2])
        rs_o = sb("rs_o", [P, 2])
        st_1 = sb("st_1", [P, 2, 6])
        mv_1 = sb("mv_1", [P, 2, 2])
        rs_1 = sb("rs_1", [P, 2])
        st_2 = sb("st_2", [P, 6])
        mv_2 = sb("mv_2", [P, 2])
        rs_2 = sb("rs_2", [P, 1])
        mneg = sb("mneg", [P, H])
        mT = sb("mT", [P, P], BF16)
        e = sb("att_e", [P, 2, 512])
        rc = sb("att_rc", [P, H])
        att = sb("att_att", [P, D])
        attT = sb("att_attT", [P, KC, P])
        res2 = sb("att_res2", [P, D])

        F0, F1, F2, BA = bank("bank_f0"), bank("bank_f1"), bank("bank_f2"), bank("bank_a")
        SB = [bank("bank_s0"), bank("bank_s1")]
        TB = [bank("bank_t0"), bank("bank_t1")]
        F2H = F2[:, 0:64].bitcast(BF16)
        BAV = BA[:, 0:H * (HD + 1)].rearrange("p (h c) -> p h c", h=H)

        a_loaded = [sem(f"a_loaded{i}") for i in range(2)]
        names = """xT_made xT_ready cT_made cT_ready zg_made th_ready on_ready onT_made ogb_ready y_ready
            zg_taken k_made k_ready v_made v_ready wout_made res1_ready x1_ready x1T_made x1T_ready q_made q_flat q_maskv q_maskg q_maska masks_seen
            var_o rstd_o var_1 rstd_1 x1b_ready s_made s_taken m_ready mt_made mt_ready t_made e_ready pv_made
            att_ready attT_made attT_ready wo_made res2_ready var_2 rstd_2 a_front a_ahead a_attn""".split()
        q = {n: sem(n) for n in names}

        def steps(eng, step):
            step(0, 0, 0, True, False)
            with eng.Fori(0, (NP - 2) // 2) as j:
                for u in range(2):
                    step(2 * j + 1 + u, (1 + u) % 2, j + u, True, True)
            step(NP - 1, 1, (NP - 2) // 2, True, True)
            step(NP, 0, NP // 2, False, True)

        def has_next(p, front):
            return front and not (isinstance(p, int) and p == NP - 1)

        with nc.Block() as block:

            @block.sync
            def _(sp):
                def load(pair, slot):
                    rows = bass.ds(2 * pair, 2)
                    for dst, src in ((xs, x_d), (cs, ctx_d), (os_, o_d)):
                        sp.dma_start(dst[:, slot], src[rows].rearrange("b t d -> t b d")).then_inc(a_loaded[slot], 16)

                load(0, 0)
                load(1, 1)
                with sp.Fori(0, (NP - 2) // 2) as j:
                    for u in range(2):
                        sp.wait_ge(q["x1_ready"], 2 * (2 * j + 1 + u))
                        load(2 * j + 2 + u, u)

            @block.tensor
            def _(pe):
                T = nc.tensor
                ident = t["ident"]
                wx = t["w_x"]
                pe.sem_inc(q["pv_made"], CR)

                def turn4(bank_, src, done):
                    for kc in range(KC):
                        for b in range(2):
                            m = T.transpose(bank_[:, (2 * kc + b) * P:(2 * kc + b + 1) * P],
                                            src[:, b, kc * P:(kc + 1) * P], ident[:])
                    m.then_inc(done, 1)

                def across(bank_, wt, rhs, done):
                    for oc in range(KC):
                        for kc in range(KC):
                            m = T.matmul(bank_[:, oc * 2 * P:(oc + 1) * 2 * P], wt[:, kc, oc * P:(oc + 1) * P],
                                         rhs[:, kc], start=(kc == 0), stop=(kc == KC - 1))
                    m.then_inc(done, 1)

                def along(bank_, lhs, wt, done):
                    for b in range(2):
                        for kc in range(KC):
                            m = T.matmul(bank_[:, b * D:(b + 1) * D], lhs[:, kc, b * P:(b + 1) * P], wt[:, kc],
                                         start=(kc == 0), stop=(kc == KC - 1))
                    m.then_inc(done, 1)

                def scores(n, s, b):
                    for g in range(4):
                        pe.wait_ge(q["s_taken"], 4 * n + g + 1)
                        for m_ in range(4):
                            h = 4 * g + m_
                            m = T.matmul(SB[g % 2][:, m_ * P:(m_ + 1) * P], qm[:, s, h // HH, b, h % HH],
                                         kT[:, s, h // HH, b * P:(b + 1) * P], start=True, stop=True)
                        m.then_inc(q["s_made"], 1)

                def shift(n):
                    pe.wait_ge(q["m_ready"], n + 1)
                    wait_if(pe, q["mt_ready"], n)
                    T.transpose(F2H, t["mparts"].rearrange("p a h -> p (a h)"), t["ident_b"][:]).then_inc(q["mt_made"], 1)

                def probs_values(n, s, b):
                    for g in range(5):
                        if g < 4:
                            pe.wait_ge(q["e_ready"], 4 * n + g + 1)
                            kc, v = g // 2, g % 2 * 4
                            T.matmul(TB[g % 2][:], kT[:, s, kc, b * P:(b + 1) * P],
                                     qm[:, s, kc, b, v:v + 4].rearrange("p h q -> p (h q)"), start=True, stop=False)
                            if g == 0:
                                pe.wait_ge(q["mt_ready"], n + 1)
                            for m_ in range(4):
                                m = T.matmul(TB[g % 2][:, m_ * P:(m_ + 1) * P], t["pick_b"][:, 4 * g + m_], mT[:],
                                             start=False, stop=(m_ == 3))
                            m.then_inc(q["t_made"], 1)
                        if g == 1:
                            pe.wait_ge(q["res2_ready"], n + 1)
                        if g >= 1:
                            pe.wait_ge(q["e_ready"], CR + 4 * n + g)
                            for m_ in range(4):
                                h = 4 * (g - 1) + m_
                                m = T.matmul(BAV[:, h], e[:, (g - 1) % 2, m_ * P:(m_ + 1) * P], t["v1"][:, s, b, h],
                                             start=True, stop=True)
                            m.then_inc(q["pv_made"], 1)

                def att_turn(n):
                    pe.wait_ge(q["att_ready"], n + 1)
                    for kc in range(KC):
                        m = T.transpose(BA[:, kc * P:(kc + 1) * P], att[:, kc * P:(kc + 1) * P], ident[:])
                    m.then_inc(q["attT_made"], 1)

                def att_out(n):
                    pe.wait_ge(q["attT_ready"], n + 1)
                    for kc in range(KC):
                        m = T.matmul(BA[:, 0:D], attT[:, kc], wx[:, 3, kc], start=(kc == 0), stop=(kc == KC - 1))
                    m.then_inc(q["wo_made"], 1)

                def step(p, s, before, front, attn):
                    n0, so = 2 * p - 2, 1 - s
                    if front:
                        pe.wait_ge(a_loaded[s], 48 * (before + 1))
                        wait_if(pe, q["x1T_ready"], p)
                        turn4(F0, xs[:, s], q["xT_made"])
                        wait_if(pe, q["q_flat"], 2 * p)
                        turn4(F1, cs[:, s], q["cT_made"])
                        pe.wait_ge(q["xT_ready"], p + 1)
                        wait_if(pe, q["mt_ready"], n0)
                        across(F2, t["w_g"], xT, q["zg_made"])
                        pe.wait_ge(q["on_ready"], 2 * p + 2)
                        turn4(F0, on, q["onT_made"])
                        pe.wait_ge(q["cT_ready"], p + 1)
                        across(F1, wx[:, 1], cT, q["k_made"])
                    if attn:
                        pe.wait_ge(q["q_maskv"], NV * KC * p)
                        pe.wait_ge(q["q_maskg"], NG * KC * p)
                        pe.wait_ge(q["q_maska"], (HH - NV - NG) * KC * p)
                        pe.wait_ge(q["k_ready"], 2 * p)
                        scores(n0, so, 0)
                    if front:
                        pe.wait_ge(q["ogb_ready"], 2 * p + 2)
                        along(F0, cT, wx[:, 2], q["v_made"])
                    if attn:
                        if front:
                            pe.wait_ge(q["zg_taken"], p + 1)
                        shift(n0)
                        pe.wait_ge(q["v_ready"], p)
                        probs_values(n0, so, 0)
                        scores(n0 + 1, so, 1)
                        att_turn(n0)
                    if front:
                        pe.wait_ge(q["y_ready"], p + 1)
                        pe.wait_ge(q["k_ready"], 2 * p + 2)
                        along(F1, yT, t["w_out"], q["wout_made"])
                    if attn:
                        att_out(n0)
                        shift(n0 + 1)
                    if attn:
                        probs_values(n0 + 1, so, 1)
                    if front:
                        pe.wait_ge(q["x1_ready"], 2 * p + 2)
                        pe.wait_ge(q["v_ready"], p + 1)
                        turn4(F0, x1, q["x1T_made"])
                    if attn:
                        att_turn(n0 + 1)
                    if front:
                        pe.wait_ge(q["x1T_ready"], p + 1)
                        across(F1, wx[:, 0], x1T, q["q_made"])
                    if attn:
                        att_out(n0 + 1)

                steps(pe, step)

            @block.scalar
            def _(act):
                A = nc.scalar
                act.sem_inc(q["e_ready"], CR)

                def flat(ap):
                    return ap.rearrange("p k n -> p (k n)")

                def shift_out(n):
                    act.wait_ge(q["mt_made"], n + 1)
                    A.activation(mT[:], F2H, ACT.Copy).then_inc(q["mt_ready"], 1)

                def exps(n):
                    for g in range(4):
                        act.wait_ge(q["t_made"], 4 * n + g + 1)
                        act.wait_ge(q["pv_made"], 4 * n + g + 1)
                        A.activation(e[:, g % 2], TB[g % 2][:], ACT.Exp).then_inc(q["e_ready"], 1)

                def att_turned(n):
                    act.wait_ge(q["attT_made"], n + 1)
                    A.activation(flat(attT), BA[:, 0:D], ACT.Copy).then_inc(q["attT_ready"], 1)

                def step(p, s, before, front, attn):
                    n0 = 2 * p - 2
                    if front:
                        act.wait_ge(q["xT_made"], p + 1)
                        A.activation(flat(xT), F0[:], ACT.Copy).then_inc(q["xT_ready"], 1)
                        act.wait_ge(q["cT_made"], p + 1)
                        A.activation(flat(cT), F1[:], ACT.Copy).then_inc(q["cT_ready"], 1)
                    if attn:
                        act.wait_ge(q["q_flat"], 2 * p)
                        for kc in range(KC):
                            for v in range(NV + NG, HH):
                                A.activation(qm[:, 1 - s, kc, :, v], qT[:, kc].rearrange("p (b n) -> p b n", b=2), ACT.Copy,
                                             scale=t["own"][:, v:v + 1]).then_inc(q["q_maska"], 1)
                    if front:
                        act.wait_ge(q["zg_made"], p + 1)
                        wait_if(act, q["zg_taken"], p)
                        A.activation(th[:], F2[:], ACT.Tanh, scale=0.5).then_inc(q["th_ready"], 1)
                        act.wait_ge(q["onT_made"], p + 1)
                        for kc in range(KC):
                            A.activation(ogb[:, kc], F0[:, kc * 2 * P:(kc + 1) * 2 * P], ACT.Identity,
                                         bias=t["beta"][:, kc:kc + 1], scale=t["gamma"][:, kc:kc + 1]).then_inc(q["ogb_ready"], 1)
                    if attn:
                        shift_out(n0)
                    if front:
                        act.wait_ge(q["k_made"], p + 1)
                        for kc in range(KC):
                            A.activation(kT[:, s, kc], F1[:, kc * 2 * P:(kc + 1) * 2 * P], ACT.Identity,
                                         bias=t["bk"][:, kc:kc + 1]).then_inc(q["k_ready"], 1)
                    if attn:
                        exps(n0)
                        att_turned(n0)
                        shift_out(n0 + 1)
                        exps(n0 + 1)
                    if front:
                        act.wait_ge(q["x1T_made"], p + 1)
                        A.activation(flat(x1T), F0[:], ACT.Copy).then_inc(q["x1T_ready"], 1)
                    if attn:
                        att_turned(n0 + 1)
                    if front:
                        act.wait_ge(q["q_made"], p + 1)
                        wait_if(act, q["q_maskv"], NV * KC * p)
                        wait_if(act, q["q_maskg"], NG * KC * p)
                        for kc in range(KC):
                            A.activation(qT[:, kc], F1[:, kc * 2 * P:(kc + 1) * 2 * P], ACT.Identity,
                                         bias=t["bq"][:, kc:kc + 1], scale=1.0 / HD ** 0.5).then_inc(q["q_flat"], 1)

                steps(act, step)

            @block.vector
            def _(dve):
                V = nc.vector
                dve.sem_inc(q["s_taken"], CR)
                dve.sem_inc(q["res2_ready"], 1)
                KF, KA = 5, 6

                def maxima(n, c):
                    for g in range(4):
                        dve.wait_ge(q["s_made"], 4 * n + g + 1)
                        V.tensor_reduce(mneg[:, 4 * g:4 * g + 4], SB[g % 2].rearrange("p (h k) -> p h k", h=4),
                                        AX.X, ALU.max, negate=True).then_inc(q["s_taken"], 1)
                    dve.wait_ge(q["s_taken"], CR + 4 * n + 4)
                    c.did(V.tensor_copy(t["mparts"][:, 0], mneg[:]))
                    c.wait()
                    V.tensor_tensor(t["mparts"][:, 1], mneg[:], t["mparts"][:, 0], ALU.subtract).then_inc(q["m_ready"], 1)

                def softmax_norm(n, c):
                    dve.wait_ge(q["pv_made"], CR + 4 * n + 4)
                    c.did(V.reciprocal(rc[:], BAV[:, :, HD]))
                    c.wait()
                    V.tensor_tensor(att.rearrange("p (h c) -> p h c", h=H), BAV[:, :, 0:HD],
                                    rc[:].unsqueeze(2).to_broadcast([P, H, HD]), ALU.mult).then_inc(q["att_ready"], 1)

                def residual(n, s, b):
                    dve.wait_ge(q["wo_made"], n + 1)
                    V.tensor_tensor(res2[:], BA[:, 0:D], x1b[:, s, b], ALU.add).then_inc(q["res2_ready"], 1)

                def finish(n, c):
                    dve.wait_ge(q["res2_ready"], n + 2)
                    c.did(V.bn_stats(st_2[:], res2[:]))
                    c.wait_apart(t["stats_seen"])
                    c.did(V.bn_aggr(mv_2[:], st_2[:]))
                    c.wait()
                    V.tensor_scalar(mv_2[:, 1:2], mv_2[:, 1:2], EPS, None, ALU.add).then_inc(q["var_2"], 1)
                    dve.wait_ge(q["rstd_2"], n + 1)
                    x2 = t["x2"][:, bass.ds(n, 1), :].rearrange("p a d -> p (a d)")
                    c.did(V.tensor_scalar(x2, res2[:], mv_2[:, 0:1], rs_2[:], ALU.subtract, ALU.mult))
                    c.wait()
                    c.did(V.tensor_reduce(t["x2_top"][:, bass.ds(n, 1)], x2, AX.X, ALU.max, apply_absolute_value=True))

                def norm(src, st, mv, rs, var, rstd, out, ready, p, c):
                    for b in range(2):
                        c.did(V.bn_stats(st[:, b], src[:, b]))
                    c.wait_apart(t["stats_seen"])
                    for b in range(2):
                        c.did(V.bn_aggr(mv[:, b], st[:, b]))
                    c.wait()
                    V.tensor_scalar(mv[:, :, 1], mv[:, :, 1], EPS, None, ALU.add).then_inc(var, 1)
                    dve.wait_ge(rstd, p + 1)
                    for b in range(2):
                        V.tensor_scalar(out[:, b], src[:, b], mv[:, b, 0:1], rs[:, b:b + 1],
                                        ALU.subtract, ALU.mult).then_inc(ready, 1)

                def norm_o(p, s, before, c):
                    dve.wait_ge(a_loaded[s], 48 * (before + 1))
                    norm(os_[:, s], st_o, mv_o, rs_o, q["var_o"], q["rstd_o"], on, q["on_ready"], p, c)

                norm_o(0, 0, 0, Chain(dve, q["a_ahead"]))

                def step(p, s, before, front, attn):
                    n0, so = 2 * p - 2, 1 - s
                    cf = Chain(dve, q["a_front"], KF * p)
                    ca = Chain(dve, q["a_attn"], KA * n0)
                    if front:
                        dve.wait_ge(q["th_ready"], p + 1)
                        V.scalar_tensor_tensor(sg[:], th[:], 1.0, F2[:], ALU.add, ALU.mult).then_inc(q["zg_taken"], 1)
                    if attn:
                        maxima(n0, ca)
                    if front:
                        dve.wait_ge(q["zg_taken"], p + 1)
                        dve.wait_ge(q["ogb_ready"], 2 * p + 2)
                        V.tensor_tensor(yT.rearrange("p k n -> p (k n)"), sg[:], ogb.rearrange("p k n -> p (k n)"),
                                        ALU.mult).then_inc(q["y_ready"], 1)
                        dve.wait_ge(q["v_made"], p + 1)
                        for b in range(2):
                            ins = V.tensor_tensor(t["v1"][:, s, b, :, 0:HD], F0[:, b * D:(b + 1) * D].rearrange("p (h c) -> p h c", h=H),
                                                  t["bv"].rearrange("p (h c) -> p h c", h=H), ALU.add)
                            if b == 0:
                                cf.did(ins)
                        ins.then_inc(q["v_ready"], 1)
                    if has_next(p, front):
                        norm_o(p + 1, 1 - s, before + s, Chain(dve, q["a_ahead"], 4 * (p + 1)))
                    if attn:
                        softmax_norm(n0, ca)
                        maxima(n0 + 1, ca)
                        residual(n0, so, 0)
                    if front:
                        dve.wait_ge(q["wout_made"], p + 1)
                        V.tensor_tensor(res1.rearrange("p b d -> p (b d)"), xs[:, s].rearrange("p b d -> p (b d)"),
                                        F1[:], ALU.add).then_inc(q["res1_ready"], 1)
                        dve.wait_ge(q["res1_ready"], p + 1)
                        wait_if(dve, q["x1b_ready"], p)
                        norm(res1, st_1, mv_1, rs_1, q["var_1"], q["rstd_1"], x1, q["x1_ready"], p, cf)
                        assert cf.n == KF, cf.n
                    if attn:
                        finish(n0, ca)
                        softmax_norm(n0 + 1, ca)
                    if front:
                        dve.wait_ge(q["q_flat"], 2 * p + 2)
                        for kc in range(KC):
                            for v in range(NV):
                                V.tensor_scalar(qm[:, s, kc, :, v], qT[:, kc].rearrange("p (b n) -> p b n", b=2),
                                                t["own"][:, v:v + 1], None, ALU.mult).then_inc(q["q_maskv"], 1)
                    if attn:
                        dve.wait_ge(q["x1b_ready"], p)
                        residual(n0 + 1, so, 1)
                        finish(n0 + 1, ca)
                        assert ca.n == 2 * KA, ca.n

                steps(dve, step)

            @block.gpsimd
            def _(pool):
                G = nc.gpsimd
                def power(var, v, mv, rs, rstd):
                    pool.wait_ge(var, v)
                    G.tensor_tensor(rs, mv, t["half_pow"][:, 0:rs.shape[1]], ALU.pow).then_inc(rstd, 1)

                def step(p, s, before, front, attn):
                    n0 = 2 * p - 2
                    if has_next(p, front):
                        power(q["var_o"], p + 2, mv_o[:, :, 1], rs_o[:], q["rstd_o"])
                    if front:
                        power(q["var_1"], p + 1, mv_1[:, :, 1], rs_1[:], q["rstd_1"])
                        pool.wait_ge(q["x1_ready"], 2 * p + 2)
                        G.tensor_tensor(x1b[:, s], x1[:], t["bo"][:].unsqueeze(1).to_broadcast([P, 2, D]),
                                        ALU.add).then_inc(q["x1b_ready"], 1)
                    if attn:
                        power(q["var_2"], n0 + 1, mv_2[:, 1:2], rs_2[:], q["rstd_2"])
                    if front:
                        pool.wait_ge(q["q_flat"], 2 * p + 2)
                        pool.sem_inc(q["masks_seen"], 1)
                        for kc in range(KC):
                            for v in range(NV, NV + NG):
                                G.tensor_scalar(qm[:, s, kc, :, v], qT[:, kc].rearrange("p (b n) -> p b n", b=2),
                                                t["own"][:, v:v + 1], 0.0, ALU.mult, ALU.add).then_inc(q["q_maskg"], 1)
                    if attn:
                        power(q["var_2"], n0 + 2, mv_2[:, 1:2], rs_2[:], q["rstd_2"])

                power(q["var_o"], 1, mv_o[:, :, 1], rs_o[:], q["rstd_o"])
                steps(pool, step)


def feedforward_block(nc, t, g_d, u_d, out_d):
    TOK = 512
    NT = B * S // TOK
    BT = TOK // S
    CR = 2
    NS = 4
    HC = FC // 2
    U = 4
    with ExitStack() as ctx:
        def sb(name, shape, dt=F32):
            return ctx.enter_context(nc.sbuf_tensor(name, shape, dt))

        def sem(name):
            return ctx.enter_context(nc.semaphore(name))

        top = sb("ff_top", [P, 2 * FC, NT])
        topr = sb("ff_topr", [P, 2 * FC])
        top1 = sb("ff_top1", [P, 2])
        topa = sb("ff_topa", [P, 2])
        sc = sb("ff_scales", [P, 16])
        cf = sb("ff_coef", [P, 2 * FC])
        early = ExitStack()
        xq = early.enter_context(nc.sbuf_tensor("ff_xq", [P, NT, 2, KC, TOK], F16))
        S_X, R_X, S_U, S_G, R_U, R_G, S_2, R_2, K_2, S_UO, R_O, K_O = range(12)

        def one(i):
            return sc[:, i:i + 1]

        banks = [ctx.enter_context(nc.psum_tensor(f"ff_bank{i}", [P, 512], F32)) for i in range(6)]
        turnb = [ctx.enter_context(nc.psum_tensor(f"ff_turn{i}", [P, 1024], F16)) for i in range(2)]

        def weights(part, kc, a, c):
            return t[part][:, ((kc * 2 + a) * FC + c) * P:((kc * 2 + a) * FC + c + 1) * P]

        def chunk_products(T, bank_, a, c, tile, done):
            terms = [(wp, xp, kc) for kc in range(KC) for wp, xp in (("w_uh", 0), ("w_uh", 1), ("w_ul", 0))]
            for i, (wp, xp, kc) in enumerate(terms):
                m = T.matmul(bank_[:], weights(wp, kc, a, c), tile[:, xp, kc],
                             start=(i == 0), stop=(i == len(terms) - 1))
            m.then_inc(done, 1)

        def low16(ap):
            return ap.bitcast(I16).rearrange("p (n two) -> p n two", two=2)[:, :, 0]

        with ExitStack() as c1:
            xr = c1.enter_context(nc.sbuf_tensor("s1_round", [P, 2, BT * D], F32))
            xh = c1.enter_context(nc.sbuf_tensor("s1_high", [P, 2, BT * D], F16))
            xl = c1.enter_context(nc.sbuf_tensor("s1_low", [P, 2, BT * D], F16))
            q = {n: c1.enter_context(nc.semaphore("s1_" + n)) for n in
                 "part all vchain split turned kept made maxed".split()}
            with nc.Block() as block:

                @block.vector
                def _(dve):
                    V = nc.vector
                    v = Chain(dve, q["vchain"])
                    v.did(V.tensor_reduce(top1[:, 0:1], t["x2_top"][:], AX.X, ALU.max))
                    v.wait()
                    dve.sem_inc(q["part"], 1)
                    dve.wait_ge(q["all"], 1)
                    v.did(V.tensor_scalar(one(S_X), topa[:, 0:1], 1.0 / QMAX, TINY, ALU.mult, ALU.max))
                    v.wait()
                    v.did(V.reciprocal(one(R_X), one(S_X)))
                    v.wait()
                    dve.sem_inc(q["maxed"], 6)
                    BASE = 3

                    def split(n, s, base):
                        w = Chain(dve, q["vchain"], base)
                        dve.wait_ge(q["turned"], 2 * n + 2)
                        w.did(V.tensor_scalar(xr[:, s], t["x2"][:, bass.ds(n * BT, BT), :].rearrange("p b d -> p (b d)"),
                                              one(R_X), MAGIC, ALU.mult, ALU.add))
                        w.wait()
                        w.did(V.tensor_scalar(xh[:, s], xr[:, s], MAGIC, None, ALU.subtract))
                        w.wait()
                        V.scalar_tensor_tensor(xl[:, s], xr[:, s], MAGIC, xh[:, s], ALU.subtract,
                                               ALU.subtract).then_inc(q["split"], 1)

                    def maxima(n):
                        for k in range(2 * FC):
                            dve.wait_ge(q["made"], n * 2 * FC + k + 1)
                            V.tensor_reduce(top[:, k, bass.ds(n, 1)], banks[k % 6][:], AX.X, ALU.max,
                                            apply_absolute_value=True).then_inc(q["maxed"], 1)

                    split(0, 0, BASE)
                    split(1, 1, BASE + 2)
                    with dve.Fori(0, (NT - 2) // 2) as j:
                        for u in range(2):
                            n = 2 * j + u
                            maxima(n)
                            split(n + 2, u, BASE + 4 + 4 * j + 2 * u)
                    maxima(NT - 2)
                    maxima(NT - 1)
                    dve.wait_ge(q["maxed"], 6 + NT * 2 * FC)
                    v = Chain(dve, q["vchain"], BASE + 2 * NT)
                    v.did(V.tensor_reduce(topr[:], top[:], AX.X, ALU.max))
                    v.wait()
                    v.did(V.tensor_tensor(topr[:], topr[:], t["top_u"][:], ALU.mult))
                    v.wait()
                    v.did(V.tensor_reduce(top1[:], topr.rearrange("p (a c) -> p a c", a=2), AX.X, ALU.max))
                    v.wait()
                    dve.sem_inc(q["part"], 1)
                    dve.wait_ge(q["all"], 2)
                    v.did(V.tensor_scalar(topa[:], topa[:], one(S_X), 1.0 / QMAX, ALU.mult, ALU.mult))
                    v.wait()
                    v.did(V.tensor_scalar(sc[:, S_U:S_G + 1], topa[:], TINY, None, ALU.max))
                    v.wait()
                    v.did(V.reciprocal(sc[:, R_U:R_G + 1], sc[:, S_U:S_G + 1]))
                    v.wait()
                    for a in range(2):
                        v.did(V.tensor_scalar(cf[:, a * FC:(a + 1) * FC], t["top_u"][:, a * FC:(a + 1) * FC],
                                              one(S_X), one(R_U + a), ALU.mult, ALU.mult))
                    v.wait()

                @block.gpsimd
                def _(pool):
                    pool.wait_ge(q["part"], 1)
                    nc.gpsimd.partition_all_reduce(topa[:, 0:1], top1[:, 0:1], P, RMAX).then_inc(q["all"], 1)
                    pool.wait_ge(q["part"], 2)
                    nc.gpsimd.partition_all_reduce(topa[:], top1[:], P, RMAX).then_inc(q["all"], 1)

                @block.tensor
                def _(pe):
                    T = nc.tensor
                    pe.sem_inc(q["turned"], 4)

                    def turn(n, s):
                        pe.wait_ge(q["split"], n + 1)
                        for part, src in ((0, xh), (1, xl)):
                            pe.wait_ge(q["kept"], 2 * n + part + 1)
                            for kc in range(KC):
                                for b in range(BT):
                                    m = T.transpose(turnb[part][:, (kc * BT + b) * P:(kc * BT + b + 1) * P],
                                                    src[:, s, b * D + kc * P:b * D + (kc + 1) * P], t["ident_h"][:])
                            m.then_inc(q["turned"], 1)

                    def products(n):
                        pe.wait_ge(q["kept"], 2 + 2 * n + 2)
                        tile = xq[:, bass.ds(n, 1)].rearrange("p a h k n -> p (a h) k n")
                        for k in range(2 * FC):
                            pe.wait_ge(q["maxed"], n * 2 * FC + k + 1)
                            chunk_products(T, banks[k % 6], k // FC, k % FC, tile, q["made"])

                    turn(0, 0)
                    with pe.Fori(0, NT // 2 - 1) as j:
                        for u in range(2):
                            turn(2 * j + u + 1, (u + 1) % 2)
                            products(2 * j + u)
                    turn(NT - 1, 1)
                    products(NT - 2)
                    products(NT - 1)

                @block.scalar
                def _(act):
                    act.sem_inc(q["kept"], 2)
                    with act.Fori(0, NT) as n:
                        for part in range(2):
                            act.wait_ge(q["turned"], 4 + 2 * n + part + 1)
                            nc.scalar.activation(xq[:, bass.ds(n, 1), part].rearrange("p a k n -> p (a k n)"),
                                                 turnb[part][:], ACT.Copy).then_inc(q["kept"], 1)

        def middle_sweep(name, a, scratch, pre):
            with ExitStack() as c2:
                def sb2(nm, shape, dt=F32):
                    return c2.enter_context(nc.sbuf_tensor(name + nm, shape, dt))

                r = sb2("round", [P, NS, TOK])
                rf = sb2("whole", [P, NS, TOK])
                other = sb2("other", [P, NS, TOK])
                ob = sb2("out", [P, 2, HC * TOK])
                ib = sb2("in", [P, 2, HC * TOK]) if pre else None
                q = {n_: c2.enter_context(nc.semaphore(name + n_)) for n_ in
                     "made seen rounded floated sigged ready backed chain outs maxed part all".split()}
                loaded, stored = ([c2.enter_context(nc.semaphore(f"{name}{n_}{i}")) for i in range(2)]
                                  for n_ in ("loaded", "stored"))

                def place(i, k):
                    return i * U + k // FC, k % FC, k % NS

                with nc.Block() as block:

                    @block.tensor
                    def _(pe):
                        with pe.Fori(0, NT) as n:
                            tile = xq[:, bass.ds(n, 1)].rearrange("p a h k n -> p (a h) k n")
                            for c in range(FC):
                                pe.wait_ge(q["rounded"], n * FC + c + 1)
                                chunk_products(nc.tensor, banks[c], a, c, tile, q["made"])

                    @block.scalar
                    def _(act):
                        A = nc.scalar

                        def sigmoid(i, k):
                            n, c, z = place(i, k)
                            act.wait_ge(q["rounded"], 6 + n * FC + c + 1)
                            act.wait_ge(q["outs"], n * FC + c + 1)
                            A.activation(other[:, z], low16(r[:, z]), ACT.Sigmoid,
                                         scale=one(S_G)).then_inc(q["sigged"], 1)

                        def floats(i, k):
                            n, c, z = place(i, k)
                            act.wait_ge(q["rounded"], 6 + n * FC + c + 1)
                            act.wait_ge(q["outs"], n * FC + c + 1)
                            A.activation(rf[:, z], r[:, z], ACT.Copy, bias=-MAGIC).then_inc(q["floated"], 1)

                        def back(i, k):
                            n, c, z = place(i, k)
                            act.wait_ge(q["ready"], n * FC + c + 1)
                            A.activation(other[:, z], other[:, z], ACT.Copy,
                                         bias=-(MAGIC if pre else MAGIC16)).then_inc(q["backed"], 1)

                        first = floats if pre else sigmoid
                        with act.Fori(0, NT // U) as i:
                            first(i, 0)
                            for k in range(U * FC):
                                if k + 1 < U * FC:
                                    first(i, k + 1)
                                back(i, k)

                    @block.gpsimd
                    def _(pool):
                        G = nc.gpsimd

                        def floats(i, k):
                            n, c, z = place(i, k)
                            pool.wait_ge(q["rounded"], 6 + n * FC + c + 1)
                            pool.wait_ge(q["outs"], n * FC + c + 1)
                            pool.sem_inc(q["seen"], 1)
                            G.tensor_scalar(rf[:, z], r[:, z], 1.0, -MAGIC, ALU.mult,
                                            ALU.add).then_inc(q["floated"], 1)

                        with pool.Fori(0, NT // U) as i:
                            if not pre:
                                floats(i, 0)
                            for k in range(U * FC):
                                n, c, z = place(i, k)
                                if not pre and k + 1 < U * FC:
                                    floats(i, k + 1)
                                if c % HC == 0:
                                    pool.wait_ge(stored[c // HC], 16 * (n + 1))
                                    pool.wait_ge(q["maxed"], n * FC + c + HC)
                                pool.wait_ge(q["floated"], n * FC + c + 1)
                                pool.wait_ge(q["backed"], n * FC + c + 1)
                                G.tensor_tensor(ob[:, c // HC, c % HC * TOK:(c % HC + 1) * TOK], other[:, z],
                                                rf[:, z], ALU.mult).then_inc(q["outs"], 1)
                        pool.wait_ge(q["part"], 1)
                        nc.gpsimd.partition_all_reduce(topa[:, 0:1], top1[:, 0:1], P, RMAX).then_inc(q["all"], 1)

                    @block.vector
                    def _(dve):
                        V = nc.vector
                        dve.sem_inc(q["rounded"], 6)
                        dve.sem_inc(q["outs"], NS)
                        dve.sem_inc(q["maxed"], FC)

                        def rounded(i, k):
                            n, c, z = place(i, k)
                            dve.wait_ge(q["made"], n * FC + c + 1)
                            dve.wait_ge(q["outs"], n * FC + c + 1)
                            V.tensor_scalar(r[:, z], banks[c][:], cf[:, a * FC + c:a * FC + c + 1], MAGIC,
                                            ALU.mult, ALU.add).then_inc(q["rounded"], 1)

                        def factor(i, k):
                            n, c, z = place(i, k)
                            if pre:
                                if c % HC == 0:
                                    dve.wait_ge(loaded[c // HC], 16 * (n + 1))
                                V.tensor_scalar(other[:, z], ib[:, c // HC, c % HC * TOK:(c % HC + 1) * TOK],
                                                one(K_2), MAGIC, ALU.mult, ALU.add).then_inc(q["ready"], 1)
                            else:
                                dve.wait_ge(q["sigged"], n * FC + c + 1)
                                V.tensor_scalar(other[:, z], other[:, z], SIG_TOP, MAGIC16,
                                                ALU.min, ALU.add).then_inc(q["ready"], 1)

                        def largest(i, k):
                            n, c, z = place(i, k)
                            dve.wait_ge(q["outs"], NS + n * FC + c + 1)
                            V.tensor_reduce(top[:, c, bass.ds(n, 1)], ob[:, c // HC, c % HC * TOK:(c % HC + 1) * TOK],
                                            AX.X, ALU.max, apply_absolute_value=True).then_inc(q["maxed"], 1)

                        with dve.Fori(0, NT // U) as i:
                            for k in range(U * FC + 4):
                                for stage, late in ((rounded, 0), (factor, 2), (largest, 4)):
                                    if 0 <= k - late < U * FC:
                                        stage(i, k - late)
                        dve.wait_ge(q["maxed"], FC + NT * FC)
                        v = Chain(dve, q["chain"])
                        v.did(V.tensor_reduce(top1[:, 0:1], top[:, 0:FC].rearrange("p c n -> p (c n)"), AX.X, ALU.max))
                        v.wait()
                        dve.sem_inc(q["part"], 1)
                        dve.wait_ge(q["all"], 1)
                        if not pre:
                            v.did(V.tensor_scalar(topa[:, 1:2], topa[:, 0:1], one(S_G), 1.0 / QMAX, ALU.mult, ALU.mult))
                            v.wait()
                            v.did(V.tensor_scalar(one(S_2), topa[:, 1:2], TINY, None, ALU.max))
                            v.wait()
                            v.did(V.reciprocal(one(R_2), one(S_2)))
                            v.wait()
                            v.did(V.tensor_scalar(one(K_2), one(R_2), one(S_G), None, ALU.mult))
                            v.wait()
                        else:
                            v.did(V.tensor_scalar(one(K_O), one(S_U), one(S_2), None, ALU.mult))
                            v.wait()
                            v.did(V.tensor_scalar(topa[:, 1:2], topa[:, 0:1], one(K_O), 1.0 / QMAX, ALU.mult, ALU.mult))
                            v.wait()
                            v.did(V.tensor_scalar(one(S_UO), topa[:, 1:2], TINY, None, ALU.max))
                            v.wait()
                            v.did(V.reciprocal(one(R_O), one(S_UO)))
                            v.wait()
                            v.did(V.tensor_scalar(one(K_O), one(K_O), one(R_O), None, ALU.mult))
                            v.wait()

                    @block.sync
                    def _(sp):
                        for s in range(2):
                            sp.sem_inc(stored[s], 16)

                        def part(d, n, s):
                            return d[bass.ds(n, 1), :, s * HC * TOK:(s + 1) * HC * TOK].rearrange("a p n -> (a p) n")

                        def load(n, s):
                            sp.dma_start(ib[:, s], part(scratch[0], n, s)).then_inc(loaded[s], 16)

                        def store(n, s):
                            sp.wait_ge(q["outs"], NS + FC * n + HC * (s + 1))
                            sp.dma_start(part(scratch[1], n, s), ob[:, s]).then_inc(stored[s], 16)

                        if pre:
                            load(0, 0)
                            load(0, 1)
                        with sp.Fori(0, NT - 1) as n:
                            for s in range(2):
                                store(n, s)
                                if pre:
                                    load(n + 1, s)
                        store(NT - 1, 0)
                        store(NT - 1, 1)
                        for s in range(2):
                            sp.wait_ge(stored[s], 16 + 16 * NT)

        middle_sweep("s2_", 1, (None, g_d), False)
        middle_sweep("s3_", 0, (g_d, u_d), True)
        early.close()

        with ExitStack() as c4:
            def sb4(nm, shape, dt=F32):
                return c4.enter_context(nc.sbuf_tensor("s4_" + nm, shape, dt))

            W = FC * TOK
            pin = sb4("in", [P, 2, W])
            whole = sb4("whole", [P, 2, W])
            halves = (slice(0, W // 2), slice(W // 2, W))
            hi = sb4("high", [P, 2, W], F16)
            lo = sb4("low", [P, 2, W], F16)
            y = sb4("y", [P, 2, BT * D])
            st = sb4("st", [P, 2, BT, 6])
            mv = sb4("mv", [P, 2, BT, 2])
            rs = sb4("rs", [P, 2, BT])
            ob = sb4("out", [P, 2, BT, D])
            q = {n_: c4.enter_context(nc.semaphore("s4_" + n_)) for n_ in
                 "rounded high floated low made scaled var rstd outs chain".split()}
            loaded, stored = ([c4.enter_context(nc.semaphore(f"s4_{n_}{i}")) for i in range(2)]
                              for n_ in ("loaded", "stored"))
            with nc.Block() as block:

                @block.sync
                def _(sp):
                    for s in range(2):
                        sp.sem_inc(stored[s], 16)

                    def load(n, s):
                        sp.dma_start(pin[:, s], u_d[bass.ds(n, 1)].rearrange("a p n -> (a p) n")).then_inc(loaded[s], 16)

                    def store(n, s):
                        sp.wait_ge(q["outs"], BT + BT * (n + 1))
                        sp.dma_start(out_d[bass.ds(n * BT, BT)].rearrange("b t d -> t b d"), ob[:, s]).then_inc(stored[s], 16)

                    load(0, 0)
                    load(1, 1)
                    for n in (0, 1):
                        sp.wait_ge(q["floated"], n + 1)
                        load(n + 2, n)
                    with sp.Fori(0, NT // 2 - 2) as j:
                        for u in range(2):
                            sp.wait_ge(q["floated"], 2 * j + u + 3)
                            load(2 * j + u + 4, u)
                            store(2 * j + u, u)
                    for n in range(NT - 4, NT):
                        store(n, n % 2)
                    for s in range(2):
                        sp.wait_ge(stored[s], 16 + 8 * NT)

                @block.scalar
                def _(act):
                    A = nc.scalar
                    with act.Fori(0, NT // 2) as j:
                        for u in range(2):
                            n = 2 * j + u
                            act.wait_ge(q["rounded"], n + 1)
                            act.wait_ge(q["low"], 2 * n + 2)
                            A.activation(whole[:, u], pin[:, u], ACT.Copy, bias=-MAGIC).then_inc(q["floated"], 1)
                            act.wait_ge(q["floated"], n + 1)
                            act.wait_ge(q["made"], 2 * n + 2)
                            for h in halves:
                                A.activation(hi[:, u, h], whole[:, u, h], ACT.Copy).then_inc(q["high"], 1)

                @block.tensor
                def _(pe):
                    T = nc.tensor
                    pe.sem_inc(q["made"], 4)
                    with pe.Fori(0, NT // 2) as j:
                        for u in range(2):
                            n = 2 * j + u
                            pe.wait_ge(q["low"], 4 + 2 * n + 2)
                            for b in range(BT):
                                bank_ = banks[2 * u + b // 2][:, b % 2 * D:(b % 2 + 1) * D]
                                if b % 2 == 0:
                                    pe.wait_ge(q["scaled"], 2 * n + b // 2 + 1)
                                i = 0
                                for c in range(FC):
                                    at = slice(c * TOK + b * S, c * TOK + (b + 1) * S)
                                    for xp, wp in ((hi, "w_dh"), (hi, "w_dl"), (lo, "w_dh")):
                                        m = T.matmul(bank_, xp[:, u, at], t[wp][:, c * D:(c + 1) * D],
                                                     start=(i == 0), stop=(i == 3 * FC - 1))
                                        i += 1
                                if b % 2 == 1:
                                    m.then_inc(q["made"], 1)

                @block.gpsimd
                def _(pool):
                    G = nc.gpsimd

                    def low(n, s):
                        for i, h in enumerate(halves):
                            pool.wait_ge(q["high"], 2 * n + i + 1)
                            G.tensor_tensor(lo[:, s, h], whole[:, s, h], hi[:, s, h], ALU.subtract).then_inc(q["low"], 1)

                    def power(n, s):
                        pool.wait_ge(q["var"], n + 1)
                        G.tensor_tensor(rs[:, s], mv[:, s, :, 1], t["half_pow"][:, 0:BT], ALU.pow).then_inc(q["rstd"], 1)

                    pool.sem_inc(q["low"], 4)
                    low(0, 0)
                    with pool.Fori(0, NT // 2 - 1) as j:
                        for u in range(2):
                            low(2 * j + u + 1, 1 - u)
                            power(2 * j + u, u)
                    low(NT - 1, 1)
                    power(NT - 2, 0)
                    power(NT - 1, 1)

                @block.vector
                def _(dve):
                    V = nc.vector
                    dve.sem_inc(q["scaled"], 4)
                    dve.sem_inc(q["outs"], BT)
                    PER = 1 + 2 * BT

                    def rounded(s, before):
                        dve.wait_ge(loaded[s], 16 * (before + 1))
                        V.tensor_scalar(pin[:, s], pin[:, s], one(K_O), MAGIC, ALU.mult, ALU.add).then_inc(q["rounded"], 1)

                    def residual(n, s):
                        c = Chain(dve, q["chain"], n * PER)
                        wait_if(dve, q["outs"], BT * n)
                        for i in range(2):
                            dve.wait_ge(q["made"], 4 + 2 * n + i + 1)
                            V.tensor_tensor(y[:, s, i * 2 * D:(i + 1) * 2 * D].rearrange("p (b d) -> p b d", b=2),
                                            banks[2 * s + i].rearrange("p (b d) -> p b d", b=2),
                                            t["top_d"][:].unsqueeze(1).to_broadcast([P, 2, D]), ALU.mult).then_inc(q["scaled"], 1)
                        dve.wait_ge(q["scaled"], 4 + 2 * n + 2)
                        c.did(V.scalar_tensor_tensor(y[:, s], y[:, s], one(S_UO),
                                                     t["x2"][:, bass.ds(n * BT, BT), :].rearrange("p b d -> p (b d)"),
                                                     ALU.mult, ALU.add))
                        c.wait()
                        for b in range(BT):
                            c.did(V.bn_stats(st[:, s, b], y[:, s, b * D:(b + 1) * D]))
                        c.wait_apart(t["stats_seen"])
                        for b in range(BT):
                            c.did(V.bn_aggr(mv[:, s, b], st[:, s, b]))
                        c.wait()
                        assert c.n == PER
                        V.tensor_scalar(mv[:, s, :, 1], mv[:, s, :, 1], EPS, None, ALU.add).then_inc(q["var"], 1)

                    def normed(n, s, before):
                        dve.wait_ge(stored[s], 16 * (before + 1))
                        dve.wait_ge(q["rstd"], n + 1)
                        for b in range(BT):
                            V.tensor_scalar(ob[:, s, b], y[:, s, b * D:(b + 1) * D], mv[:, s, b, 0:1], rs[:, s, b:b + 1],
                                            ALU.subtract, ALU.mult).then_inc(q["outs"], 1)

                    def step(n, s, before, first=False, last=False):
                        if not last:
                            rounded(s, before + 1)
                        residual(n, s)
                        if not first:
                            normed(n - 1, 1 - s, before - 1 + s)

                    rounded(0, 0)
                    rounded(1, 0)
                    step(0, 0, 0, first=True)
                    with dve.Fori(0, NT // 2 - 2) as j:
                        for u in range(2):
                            step(2 * j + 1 + u, 1 - u, j + u)
                    step(NT - 3, 1, NT // 2 - 2)
                    step(NT - 2, 0, NT // 2 - 1, last=True)
                    step(NT - 1, 1, NT // 2 - 1, last=True)
                    normed(NT - 1, 1, NT // 2 - 1)


def decoder_layer(nc, x_d, ctx_d, w, out_d):
    with ExitStack() as ctx:
        def sb(name, shape, dt=F32):
            return ctx.enter_context(nc.sbuf_tensor(name, shape, dt))

        NT = B * S // 512
        stats_seen = ctx.enter_context(nc.semaphore("stats_seen"))
        o_d = nc.dram_tensor("rec_scratch", (B, S, D), F32).ap()
        g_d = nc.dram_tensor("gate_scratch", (NT, P, FC * 512), F32).ap()
        u_d = nc.dram_tensor("product_scratch", (NT, P, FC * 512), F32).ap()
        t = {
            "ident": sb("ident", [P, P]), "ident_b": sb("ident_b", [P, P], BF16), "ident_h": sb("ident_h", [P, P], F16),
            "half_pow": sb("half_pow", [P, 4]), "stats_seen": stats_seen,
            "w_uh": sb("w_uh", [P, KC * 2 * FC * P], F16), "w_ul": sb("w_ul", [P, KC * 2 * FC * P], F16),
            "w_dh": sb("w_dh", [P, FC * D], F16), "w_dl": sb("w_dl", [P, FC * D], F16),
            "top_u": sb("top_u", [P, 2 * FC]), "top_d": sb("top_d", [P, D]),
            "x2": sb("x2", [P, B, D]), "x2_top": sb("x2_top", [P, B]),
        }
        with ExitStack() as early:
            def se(name, shape, dt=F32):
                return early.enter_context(nc.sbuf_tensor(name, shape, dt))

            t.update({
                "own": se("own", [P, HH]), "mparts": se("mparts", [P, P // H, H], BF16), "pick": se("pick", [P, H]), "pick_b": se("pick_b", [P, H, P], BF16),
                "ones64": se("ones64", [1, B]),
                "w_rec": se("w_rec", [P, KC, HALF, 4, P]),
                "bf_row": se("bf_row", [1, D]),
                "w_g": se("w_g", [P, KC, D]), "w_out": se("w_out", [P, KC, D]),
                "w_x": se("w_x", [P, 4, KC, D]),
                "gamma": se("gamma", [P, KC]), "beta": se("beta", [P, KC]),
                "bq": se("bq", [P, KC]), "bk": se("bk", [P, KC]),
                "bv": se("bv", [P, D]), "bo": se("bo", [P, D]),
                "v1": se("v1", [P, 2, 2, H, HD + 1]),
            })
            setup_block(nc, t, w)
            recurrence_block(nc, t, x_d, o_d)
            attention_block(nc, t, x_d, ctx_d, o_d)
        feedforward_block(nc, t, g_d, u_d, out_d)


NAMES = {
    "q": "L0_attn_Wq", "k": "L0_attn_Wk", "v": "L0_attn_Wv", "f": "L0_attn_Wf", "bf": "L0_attn_bf",
    "g": "L0_attn_Wg", "out": "L0_attn_Wout", "gamma": "L0_attn_gamma", "beta": "L0_attn_beta",
    "xq": "L0_xattn_Wq", "bq": "L0_xattn_bq", "xk": "L0_xattn_Wk", "bk": "L0_xattn_bk",
    "xv": "L0_xattn_Wv", "bv": "L0_xattn_bv", "xo": "L0_xattn_Wo", "bo": "L0_xattn_bo",
    "gate": "L0_ffn_w_gate", "up": "L0_ffn_w_up", "down": "L0_ffn_w_down",
}


def kernel(**inputs):
    import numpy as np
    import concourse.bacc as bacc
    from concourse.bass_utils import run_bass_kernel_spmd as run

    nc = bacc.Bacc("TRN2", target_bir_lowering=False, num_devices=1)
    arrays, aps = {}, {}
    for short, name in {"x": "x", "ctx": "ctx_1024", **NAMES}.items():
        a = np.ascontiguousarray(inputs[name])
        arrays[f"in_{short}"] = a
        aps[short] = nc.dram_tensor(f"in_{short}", a.shape, mybir.dt.from_np(a.dtype), kind="ExternalInput").ap()
    out = nc.dram_tensor("out_0", (B, S, D), F32, kind="ExternalOutput").ap()
    decoder_layer(nc, aps["x"], aps["ctx"], aps, out)
    r = run(nc, [arrays], core_ids=[0])
    return r.results[0]["out_0"]
```
